# Optimizing a Trainium2 kernel written in Bass

```python
import numpy as np
import jax
import jax.numpy as jnp

def _softmax(x, axis=-1):
    return jax.nn.softmax(x, axis=axis)

def _gelu(x):
    return jax.nn.gelu(x, approximate=True)

def _silu(x):
    return jax.nn.silu(x)

def _sigmoid(x):
    return jax.nn.sigmoid(x)

def _layernorm(x, axis=-1, eps=1e-05):
    m = jnp.mean(x, axis=axis, keepdims=True)
    v = jnp.var(x, axis=axis, keepdims=True)
    return (x - m) / jnp.sqrt(v + eps)

def _scatter_add(tgt, idx, src, axis=0):
    return tgt.at[idx].add(src)

def _segment_sum(src, seg, n):
    return jax.ops.segment_sum(src, seg, n)
kernel_name = 'mk_gps_d1_gnn_r8_c28eea'

def setup_inputs(seed: int=0):
    np.random.seed(seed)
    _w = jnp.asarray

    def _rec_inputs():
        import jax
        import jax.numpy as jnp
        _gk = jax.random.key(seed)
        x = -8.776e-05 + 1 * jax.random.normal(jax.random.fold_in(_gk, 1), (1250, 1024), jnp.float32)
        src = jax.random.randint(jax.random.fold_in(_gk, 2), (40000,), 0, 1250, jnp.int32)
        dst = jax.random.randint(jax.random.fold_in(_gk, 3), (40000,), 0, 1250, jnp.int32)
        _o = jnp.argsort(dst, stable=True)
        src = src[_o]
        dst = dst[_o]
        return (x, src, dst)
    x, src, dst = _rec_inputs()

    def _L0_gnn_setup():
        import math
        import jax, jax.numpy as jnp
        import numpy as np
        N_NODES = 625
        N_EDGES = 20000
        D_IN = 1024
        D_OUT = 1024
        BN_EPS = 1e-05

        def _positional_encoding(n, d):
            pos = jnp.arange(n, dtype=jnp.float32)[:, None]
            div = jnp.exp(jnp.arange(0, d, 2, dtype=jnp.float32) * (-math.log(10000.0) / d))
            ang = pos * div
            pe = jnp.stack([jnp.sin(ang), jnp.cos(ang)], axis=-1).reshape(n, d)
            return pe

        def _gcn_conv(x, W, b, src, dst, dinv):
            xw = x @ W
            norm = (dinv[src] * dinv[dst])[:, None]
            agg = jax.ops.segment_sum(xw[src] * norm, dst, num_segments=x.shape[0])
            agg = agg + xw * (dinv * dinv)[:, None]
            return agg + b
        key = jax.random.key(seed)
        ks = jax.random.split(key, 8)
        x = jax.random.normal(ks[0], (N_NODES, D_IN), dtype=jnp.float32)
        src = jax.random.randint(ks[1], (N_EDGES,), 0, N_NODES, dtype=jnp.int32)
        dst = jax.random.randint(ks[2], (N_EDGES,), 0, N_NODES, dtype=jnp.int32)
        s1 = 1.0 / math.sqrt(D_IN)
        s2 = 1.0 / math.sqrt(D_OUT)
        W1 = jax.random.uniform(ks[3], (D_IN, D_OUT), jnp.float32, -s1, s1)
        b1 = jnp.zeros((D_OUT,), jnp.float32)
        gamma = jnp.ones((D_OUT,), jnp.float32)
        beta = jnp.zeros((D_OUT,), jnp.float32)
        W2 = jax.random.uniform(ks[4], (D_OUT, D_OUT), jnp.float32, -s2, s2)
        b2 = jnp.zeros((D_OUT,), jnp.float32)
        return {'x': x, 'src': src, 'dst': dst, 'W1': W1, 'b1': b1, 'gamma': gamma, 'beta': beta, 'W2': W2, 'b2': b2}
    _L0_gnn_all = _L0_gnn_setup()
    _L0_gnn_in = {k: v for k, v in _L0_gnn_all.items() if k in ('W1', 'b1', 'gamma', 'beta', 'W2', 'b2')}
    del _L0_gnn_all

    def _L0_mix_setup():
        import jax, jax.numpy as jnp
        import numpy as np
        B, S, D = (4, 512, 1024)
        H, DH, F = (16, 64, 256)
        EPS = 1e-08
        key = jax.random.key(seed)
        ks = jax.random.split(key, 7)
        return {'hidden_states': jax.random.normal(ks[0], (B, S, D), dtype=jnp.float32), 'Wq': jax.random.normal(ks[1], (D, D), dtype=jnp.float32) / np.sqrt(D), 'Wk': jax.random.normal(ks[2], (D, D), dtype=jnp.float32) / np.sqrt(D), 'Wv': jax.random.normal(ks[3], (D, D), dtype=jnp.float32) / np.sqrt(D), 'proj': jax.random.normal(ks[4], (DH, F), dtype=jnp.float32) / np.sqrt(DH), 'Wo': jax.random.normal(ks[5], (D, D), dtype=jnp.float32) / np.sqrt(D), 'bo': jnp.zeros((D,), dtype=jnp.float32)}
    _L0_mix_all = _L0_mix_setup()
    _L0_mix_in = {k: v for k, v in _L0_mix_all.items() if k in ('Wq', 'Wk', 'Wv', 'proj', 'Wo', 'bo')}
    del _L0_mix_all

    def _L0_ffn_setup():
        import jax, jax.numpy as jnp
        import numpy as np
        B, T, C = (4, 256, 1024)
        E, F, K = (8, 256, 2)
        key = jax.random.key(seed)
        k0, k1, k2, k3 = jax.random.split(key, 4)
        s = lambda d: 1.0 / np.sqrt(d)
        x = jax.random.normal(k0, (B, T, C), dtype=jnp.float32)
        Wr = jax.random.normal(k1, (E, C), dtype=jnp.float32) * s(C)
        W1 = jax.random.normal(k2, (E, 2 * F, C), dtype=jnp.float32) * s(C)
        W2 = jax.random.normal(k3, (E, C, F), dtype=jnp.float32) * s(F)
        return {'x': x, 'Wr': Wr, 'W1': W1, 'W2': W2}
    _L0_ffn_all = _L0_ffn_setup()
    _L0_ffn_in = {k: v for k, v in _L0_ffn_all.items() if k in ('Wr', 'W1', 'W2')}
    del _L0_ffn_all
    return {'x': x, 'src': src, 'dst': dst, 'L0_gnn_W1': _L0_gnn_in['W1'], 'L0_gnn_b1': _L0_gnn_in['b1'], 'L0_gnn_gamma': _L0_gnn_in['gamma'], 'L0_gnn_beta': _L0_gnn_in['beta'], 'L0_gnn_W2': _L0_gnn_in['W2'], 'L0_gnn_b2': _L0_gnn_in['b2'], 'L0_mix_Wq': _L0_mix_in['Wq'], 'L0_mix_Wk': _L0_mix_in['Wk'], 'L0_mix_Wv': _L0_mix_in['Wv'], 'L0_mix_proj': _L0_mix_in['proj'], 'L0_mix_Wo': _L0_mix_in['Wo'], 'L0_mix_bo': _L0_mix_in['bo'], 'L0_ffn_Wr': _L0_ffn_in['Wr'], 'L0_ffn_W1': _L0_ffn_in['W1'], 'L0_ffn_W2': _L0_ffn_in['W2']}

def reference(x, src, dst, L0_gnn_W1, L0_gnn_b1, L0_gnn_gamma, L0_gnn_beta, L0_gnn_W2, L0_gnn_b2, L0_mix_Wq, L0_mix_Wk, L0_mix_Wv, L0_mix_proj, L0_mix_Wo, L0_mix_bo, L0_ffn_Wr, L0_ffn_W1, L0_ffn_W2):
    import jax
    import jax.numpy as jnp

    def _L0_gnn_ref(x, src, dst, W1, b1, gamma, beta, W2, b2):
        import math
        import jax, jax.numpy as jnp
        import numpy as np
        N_NODES = 625
        N_EDGES = 20000
        D_IN = 1024
        D_OUT = 1024
        BN_EPS = 1e-05

        def _positional_encoding(n, d):
            pos = jnp.arange(n, dtype=jnp.float32)[:, None]
            div = jnp.exp(jnp.arange(0, d, 2, dtype=jnp.float32) * (-math.log(10000.0) / d))
            ang = pos * div
            pe = jnp.stack([jnp.sin(ang), jnp.cos(ang)], axis=-1).reshape(n, d)
            return pe

        def _gcn_conv(x, W, b, src, dst, dinv):
            xw = x @ W
            norm = (dinv[src] * dinv[dst])[:, None]
            agg = jax.ops.segment_sum(xw[src] * norm, dst, num_segments=x.shape[0])
            agg = agg + xw * (dinv * dinv)[:, None]
            return agg + b
        n = x.shape[0]
        x = x + _positional_encoding(n, x.shape[1])
        deg = jax.ops.segment_sum(jnp.ones_like(dst, dtype=x.dtype), dst, num_segments=n) + 1.0
        dinv = deg ** (-0.5)
        h = _gcn_conv(x, W1, b1, src, dst, dinv)
        mu = h.mean(axis=0)
        var = h.var(axis=0)
        h = (h - mu) * jax.lax.rsqrt(var + BN_EPS) * gamma + beta
        h = jax.nn.relu(h)
        h = _gcn_conv(h, W2, b2, src, dst, dinv)
        return jax.nn.relu(h)

    def _L0_mix_ref(hidden_states, Wq, Wk, Wv, proj, Wo, bo):
        import jax, jax.numpy as jnp
        import numpy as np
        B, S, D = (4, 512, 1024)
        H, DH, F = (16, 64, 256)
        EPS = 1e-08
        b, s, _ = hidden_states.shape

        def heads(x):
            return x.reshape(b, s, H, DH).transpose(0, 2, 1, 3)
        q = heads(hidden_states @ Wq)
        k = heads(hidden_states @ Wk)
        v = heads(hidden_states @ Wv)
        q_prime = jax.nn.relu(q @ proj)
        k_prime = jax.nn.relu(k @ proj)
        kv = jnp.einsum('bhsf,bhsd->bhfd', k_prime, v)
        attn = jnp.einsum('bhsf,bhfd->bhsd', q_prime, kv)
        norm = jnp.einsum('bhsf,bhf->bhs', q_prime, k_prime.sum(axis=2))[..., None]
        attn = attn / (norm + EPS)
        attn = attn.transpose(0, 2, 1, 3).reshape(b, s, D)
        return attn @ Wo + bo

    def _L0_ffn_ref(x, Wr, W1, W2):
        import jax, jax.numpy as jnp
        import numpy as np
        B, T, C = (4, 256, 1024)
        E, F, K = (8, 256, 2)
        Bb, Tt, Cc = x.shape
        flat = x.reshape(-1, Cc)
        N = flat.shape[0]
        logits = flat @ Wr.T
        weights, ids = jax.lax.top_k(logits, K)
        weights = jax.nn.softmax(weights, axis=-1)
        rows = jnp.arange(N)[:, None]
        router_weights = jnp.zeros((N, E), dtype=flat.dtype).at[rows, ids].add(weights)
        h = jnp.einsum('nc,efc->nef', flat, W1)
        val, gate = (h[..., :F], h[..., F:])
        act = val * jax.nn.silu(gate)
        expert_outputs = jnp.einsum('nef,ecf->nec', act, W2)
        out = jnp.einsum('nec,ne->nc', expert_outputs, router_weights)
        return out.reshape(Bb, Tt, Cc)
    xn = _layernorm(x, axis=-1)
    x = x + _L0_gnn_ref(xn, src, dst, L0_gnn_W1, L0_gnn_b1, L0_gnn_gamma, L0_gnn_beta, L0_gnn_W2, L0_gnn_b2) + _L0_mix_ref(xn[None], L0_mix_Wq, L0_mix_Wk, L0_mix_Wv, L0_mix_proj, L0_mix_Wo, L0_mix_bo)[0]
    x = x + _L0_ffn_ref(_layernorm(x, axis=-1)[None], L0_ffn_Wr, L0_ffn_W1, L0_ffn_W2)[0]
    return x

_drawn_inputs = setup_inputs


def setup_inputs(seed=0):
    import zlib

    import numpy as np

    out = dict(_drawn_inputs(seed))
    spreads = {'L0_gnn_b1': (0.0, 0.1),
     'L0_gnn_gamma': (1.0, 0.2),
     'L0_gnn_beta': (0.0, 0.1),
     'L0_gnn_b2': (0.0, 0.1),
     'L0_mix_bo': (0.0, 0.1)}
    factors = {}
    for name, (base, spread) in spreads.items():
        noise = np.random.default_rng([zlib.crc32(name.encode()), seed]).standard_normal(out[name].shape)
        drawn = base * np.exp(spread * noise) if base else spread * noise
        out[name] = jnp.asarray(drawn.astype(out[name].dtype))
    for name, factor in factors.items():
        out[name] = (out[name] * factor).astype(out[name].dtype)
    return out
```

```python
from contextlib import ExitStack

import numpy as np

import concourse.bass as bass
from concourse import mybir


F32 = mybir.dt.float32
F32R = mybir.dt.float32r
BF16 = mybir.dt.bfloat16
F16 = mybir.dt.float16
I32 = mybir.dt.int32
ALU = mybir.AluOpType
ACT = mybir.ActivationFunctionType
AX = mybir.AxisListType

N, D = 1250, 1024
T = 125
NT = N // T
KD = D // 128
CW = 418
NP = 3 * CW
NE = 40000
CH = 125
NCH = NE // CH
GC = 4
NG = NCH // GC
HEADS, DH, FEAT = 16, 64, 256
PAIRS = HEADS // 2
EXP, FF = 8, 256
BN_EPS, LN_EPS, ATT_EPS = 1e-5, 1e-5, 1e-8
COMBOS = ((0, 0), (0, 1), (1, 0))


def slab_steps():
    s = [("H", 1, f) for f in range(KD)] + [("H", 2, f) for f in range(KD)]
    s += [("V", 0), ("K", 0), ("Q", 0)]
    for p in range(1, PAIRS):
        s += [("K", p), ("Q", p), ("V", p)]
    s += [("O", f) for f in range(KD)]
    for e in range(EXP):
        s += [("GA", e, 0), ("VA", e, 0), ("GA", e, 1), ("VA", e, 1)]
    return s


SLABS = slab_steps()
SLAB = {k: n for n, k in enumerate(SLABS)}


def steps():
    o = [("LNA",)]
    for b in range(NT):
        o.append(("G", b))
        if b == 3:
            o.append(("LNS",))
            o += [("LNB", i) for i in range(2)]
        if 4 <= b < 8:
            o += [("LNB", i) for i in range(2 * b - 6, 2 * b - 4)]
        if b:
            o.append(("GT", b - 1))
    o += [("GT", NT - 1), ("DEG",), ("DB",)]

    def with_split(key):
        n = SLAB[key] + 1
        return ([("P", n)] if n < len(SLABS) else []) + [key]

    for layer in (1, 2):
        o += [("ZP", layer, 0)]
        for t in range(KD):
            if t + 1 < KD:
                o.append(("ZP", layer, t + 1))
            if t == KD - 1 and layer == 1:
                o.append(("P", 0))
            o.append(("Z", layer, t))
        for f in range(KD):
            o += with_split(("H", layer, f))
            if layer == 1 and f:
                o.append(("HT", f - 1))
        if layer == 1:
            o.append(("HT", KD - 1))
    o += [("XT", i) for i in range(NT)] + [("MP",)]
    o += with_split(("V", 0)) + with_split(("K", 0)) + [("VT", 0)] + with_split(("Q", 0))
    for p in range(PAIRS):
        more = p + 1 < PAIRS
        o += [("KK", p, 0)]
        for i in range(1, NT):
            o += [("KK", p, i), ("KV", p, i - 1)]
        o += [("KV", p, NT - 1), ("QP", p, 0, 0), ("KC", p), ("QP", p, 0, 1), ("S", p)]
        o += with_split(("K", p + 1)) if more else []
        o += [("AT", p, 0), ("QP", p, 1, 0), ("QP", p, 1, 1)]
        o += with_split(("Q", p + 1)) if more else []
        o += [("AT", p, 1), ("RC", p)]
        o += with_split(("V", p + 1)) + [("VT", p + 1)] if more else []
    o += [("AP", k) for k in range(KD)]
    for f in range(KD):
        o += with_split(("O", f))
        if f:
            o.append(("OT", f - 1))
    o += [("OT", KD - 1), ("LN2",), ("FL", 0)]
    for j in range(NT):
        if j + 1 < NT:
            o.append(("FL", j + 1))
        o.append(("FT", j))
    o += [("R",), ("RT",), ("W2P", 0)]
    for e in range(EXP):
        o += with_split(("GA", e, 0))
        if e:
            o += [("OUT", e - 1, j) for j in range(NT)] + [("W2P", e)]
        for key in (("VA", e, 0), ("GA", e, 1), ("VA", e, 1)):
            o += with_split(key)
    o += [("OUT", EXP - 1, j) for j in range(NT)]
    return o


ORDER = steps()
PSUM_KINDS = {"G", "GT", "DB", "Z", "H", "HT", "XT", "V", "VT", "K", "Q", "KK", "QP", "AT",
              "O", "OT", "FT", "R", "RT", "S", "GA", "VA", "OUT"}
ACT_KINDS = PSUM_KINDS - {"O", "OT", "OUT"} | {"P", "ZP", "KC", "AP", "W2P", "LNB", "MP"}
DVE_KINDS = {"ZP", "Z", "P", "XT", "VT", "K", "Q", "KK", "S", "QP", "RC", "AP", "O", "OT",
             "FL", "FT", "RT", "W2P", "MP", "VA", "OUT"}


def numbered(kinds):
    return {k: n + 1 for n, k in enumerate(k for k in ORDER if k[0] in kinds)}


FULL = numbered(PSUM_KINDS)
ACTED = numbered(ACT_KINDS)
DVED = numbered(DVE_KINDS)


def slot_of(key):
    return (FULL[key] - 1) % 2


def freed(key):
    return (FULL[key] - 1) // 2 + 1


def build(nc, x, src_cols, dst_cols, dst_groups, slabs, w2, wr, proj, feat_rows, consts, group_no, tie,
          iota, pe, out):
    ctx = ExitStack()
    with ctx:
        sem = lambda name: ctx.enter_context(nc.semaphore(name))
        small = lambda name, shape, dt=F32: ctx.enter_context(nc.sbuf_tensor(name, shape, dt))

        ident = small("ident", [128, 128])
        onesf = small("onesf", [128, 128])
        zeros = small("zeros", [128, 128], BF16)
        eps = small("eps", [128, 1])
        rows = small("rows", [128, 5 * KD])
        b1c, gammac, betac, b2c, boc = (rows[:, KD * i:KD * i + KD] for i in range(5))
        wr_p = [small(f"wr_{n}", [128, (KD - 1) * 2 * EXP + 128], F32R) for n in ("hilo", "hi0")]
        gno = small("gno", [NG, 2])
        tile_no = small("tile_no", [NG, 2 * NT])
        gmm = small("gmm", [NG, 2])
        key_a = small("key_a", [NG, NT])
        key_b = small("key_b", [NG, 2 * NT])
        key_m = small("key_m", [NG, 2 * NT])
        lims = small("lims", [1, 6 * NT])
        bounds = small("bounds", [1, 3 * NT], I32)
        degs = small("degs", [T, 2 * NT])
        dinv = small("dinv", [T, NT])
        nw = small("nw", [128, 6 * NT])
        xsum = small("xsum", [T, NT])
        nmean = small("nmean", [T, NT])
        vsum = small("vsum", [T, NT])
        std = small("std", [128, NT])
        rstd = small("rstd", [T, NT])
        bst = small("bst", [128, 3 * 6])
        bmv = small("bmv", [128, 2])
        bsc = small("bsc", [128, 2])
        l2st = small("l2st", [T, 2 * 6])
        l2mv = small("l2mv", [T, 2 * NT])
        rw = small("rw", [T, NT * EXP])

        base = (nc.sbuf_base + 31) // 32 * 32

        def at(name, off, shape, dt=F32):
            return nc.alloc_sbuf_tensor_at(name, shape, dt, offset=base + off)

        BIG = 2 * KD * NP * 4
        big = [at("big_hi", 0, [128, KD, NP], F32R), at("big_lo", BIG // 2, [128, KD, NP], F32R)]
        slab_raw = [at(f"slab_raw{s}", BIG + 4096 * s, [128, KD * 128]) for s in range(2)]
        slab_p = [[at(f"slab_{'hl'[q]}{s}", BIG + 8192 + 8192 * s + 4096 * q, [128, KD, 128], F32R)
                   for q in range(2)] for s in range(2)]
        R = BIG + 24576
        wr_raw = at("wr_raw", BIG + 8192 + 12288, [128, KD * EXP])
        dx = at("dx", 0, [T, NT, D])
        xt = [at(f"xt{s}", 40960 + 4096 * s, [T, D]) for s in range(2)]
        xn = [at(f"xn{s}", 49152 + 4096 * s, [T, D]) for s in range(2)]
        grp_i = at("grp_i", 49152, [NG, GC * CH], I32)
        grp_f = at("grp_f", 51168, [NG, GC * CH])
        iota_t = at("iota_t", 57344, [T, N], F16)
        oh_src = [at(f"oh_src{j}", 59872 + 2528 * j, [T, N], BF16) for j in range(GC)]
        oh_dst = [at(f"oh_dst{j}", 69984 + 256 * j, [T, T], BF16) for j in range(GC)]
        srcf = at("srcf", 71008, [CH, NCH])
        dstf = at("dstf", 72288, [CH, NCH])
        srci = at("srci", 73568, [CH, NCH], I32)
        dsti = at("dsti", 74848, [CH, NCH], I32)
        adj = at("adj", R, [T, NT, NP], F32R)
        XS = R + 50176
        xs_raw = [at(f"xs_raw{s}", XS + 5120 * s, [T, NT, 128]) for s in range(2)]
        xs_p = [[at(f"xs_{'hl'[q]}{s}", XS + 10240 + 10240 * s + 5120 * q, [T, NT, 128], F32R)
                 for q in range(2)] for s in range(2)]
        pet = [at(f"pet{s}", XS + 4096 * s, [T, D]) for s in range(2)]
        x0t = [at(f"x0t{s}", XS + 8192 + 4096 * s, [T, D]) for s in range(2)]
        ZT = XS + 30720
        ztmp = [at(f"ztmp{s}", ZT + 5024 * s, [128, NP]) for s in range(2)]
        htmp = [at(f"htmp{s}", ZT + 5024 * s, [128, NP]) for s in range(2)]
        cnt = [at(f"cnt{s}", ZT + 5024 * s, [T, N]) for s in range(2)]
        hout = at("hout", ZT + 10048, [T, NT * 128])
        diag = at("diag", ZT + 10048, [T, NT, T])
        dinv_b = at("dinv_b", ZT + 10048 + 5120, [128, NP])
        q_p = [at(f"qT_{'hl'[q]}", R + 5024 * q, [128, NP], F32R) for q in range(2)]
        k_p = [at(f"kT_{'hl'[q]}", R + 10048 + 5024 * q, [128, NP], F32R) for q in range(2)]
        vt = at("vT", R + 20096, [128, NP])
        v_p = [at(f"v_{'hl'[q]}", R + 25120 + 10240 * q, [T, NT, 256], F32R) for q in range(2)]
        qp_p = [at(f"qp_{'hl'[q]}", R + 45600 + 10048 * q, [128, 2, NP], F32R) for q in range(2)]
        xn_in = [at(f"xn_in{s}", R + 45600 + 4096 * s, [T, D]) for s in range(2)]
        kk_p = [[at(f"kk_{'hl'[q]}{s}", R + 65696 + 4096 * s + 2048 * q, [T, 2 * FEAT], F32R)
                 for q in range(2)] for s in range(2)]
        s_p = [at(f"s_{'hl'[q]}", R + 73888 + 2048 * q, [128, 2, 2, 128], F32R) for q in range(2)]
        num = at("num", R + 77984, [128, NP])
        nrm = at("nrm", R + 83008, [128, NP])
        att = at("att", R + 88032, [128, NP])
        proj_raw = at("proj_raw", R + 93056, [128, 2 * FEAT])
        proj_p = [at(f"proj_{'hl'[q]}", R + 95104 + 2048 * q, [128, 2 * FEAT], F32R) for q in range(2)]
        kvt = at("kvt", R + 99200, [128, 2 * FEAT])
        acc = at("acc", R, [T, NT, D])
        gnn_in = [at(f"gnn_in{s}", R + 40960 + 5024 * s, [128, NP]) for s in range(2)]
        otmp = [at(f"otmp{s}", R + 51008 + 5024 * s, [128, NP]) for s in range(2)]
        x_in = [at(f"x_in{s}", R + 61056 + 5120 * s, [T, NT, 128]) for s in range(2)]
        at_in = [at(f"at_in{s}", R + 71296 + 5024 * s, [128, NP]) for s in range(2)]
        flat = [at(f"flat{s}", R + 40960 + 4096 * s, [T, D]) for s in range(2)]
        a_p = [at(f"a_{'hl'[q]}", R + 40960 + 10048 * q, [128, 2, NP], F32R) for q in range(2)]
        sil = at("sil", R + 61056, [128, NP])
        actt = at("actt", R + 66080, [128, NP])
        w2_raw = at("w2_raw", R + 71104, [128, 2, D])
        w2_p = [at(f"w2_{'hl'[q]}", R + 79296 + 8192 * q, [128, 2, D], F32R) for q in range(2)]
        lg = at("lg", R + 61056, [T, NT, EXP])
        lgt = at("lgt", R + 40960, [2 * EXP, NP])
        lg2 = at("lg2", R + 45984, [T, NT * 2 * EXP])
        cmp_gt = at("cmp_gt", R + 61376, [T, NT, EXP * EXP])
        cmp_ge = at("cmp_ge", R + 66080, [T, NT, EXP * EXP])
        tie_t = at("tie_t", R + 95680, [T, EXP * EXP])
        rank = at("rank", R + 95936, [T, NT, EXP])
        rsm = at("rsm", R + 96256, [T, 8 * NT])
        rtmp = at("rtmp", R + 96576, [T, NT, EXP])

        slot = [ctx.enter_context(nc.psum_tensor(f"slot{s}", [128, 1536], F32)) for s in range(2)]
        kvb = ctx.enter_context(nc.psum_tensor("kvb", [128, 512], F32))

        xn_d = nc.dram_tensor("xn_d", [N, D], F32, kind="Internal").ap()
        xs_d = [nc.dram_tensor(f"xs_d{i}", [KD, T, NT * 128], F32, kind="Internal").ap() for i in range(2)]
        gnn_d = nc.dram_tensor("gnn_d", [KD, 128, NP], F32, kind="Internal").ap()
        at_d = nc.dram_tensor("at_d", [KD, 128, NP], F32, kind="Internal").ap()

        const_in = sem("const_in")
        edges_in = sem("edges_in")
        memset_done = sem("memset_done")
        chain = sem("chain")
        bounds_ready = sem("bounds_ready")
        keys_ready = sem("keys_ready")
        keys_max = sem("keys_max")
        oh_ready = [sem(f"oh_ready{j}") for j in range(GC)]
        oh_used = [sem(f"oh_used{j}") for j in range(GC)]
        diag_added = sem("diag_added")
        x_landed = [sem(f"x_landed{s}") for s in range(2)]
        x_used = sem("x_used")
        achain = sem("achain")
        ln_sums = sem("ln_sums")
        rstd_ready = sem("rstd_ready")
        xn_stored = [sem(f"xn_stored{s}") for s in range(2)]
        pe_landed = [sem(f"pe_landed{s}") for s in range(2)]
        x0_ready = sem("x0_ready")
        x0_stored = [sem(f"x0_stored{s}") for s in range(2)]
        deg_sqrt = sem("deg_sqrt")
        diag_ready = sem("diag_ready")
        dinv_ready = sem("dinv_ready")
        slab_landed = [sem(f"slab_landed{s}") for s in range(2)]
        xs_landed = [sem(f"xs_landed{s}") for s in range(2)]
        xs_scaled = sem("xs_scaled")
        z_scaled = sem("z_scaled")
        h_biased = sem("h_biased")
        bn_ready = sem("bn_ready")
        std_ready = sem("std_ready")
        bn_affine = sem("bn_affine")
        h_stored = sem("h_stored")
        gnn_stored = [sem(f"gnn_stored{s}") for s in range(2)]
        xn_landed = [sem(f"xn_landed{s}") for s in range(2)]
        kv_full = sem("kv_full")
        att_stored = sem("att_stored")
        at_landed = [sem(f"at_landed{s}") for s in range(2)]
        gnn_landed = [sem(f"gnn_landed{s}") for s in range(2)]
        xr_landed = [sem(f"xr_landed{s}") for s in range(2)]
        ln2_var = sem("ln2_var")
        ln2_std = sem("ln2_std")
        exp_in = sem("exp_in")
        exp_out = sem("exp_out")
        w2_landed = sem("w2_landed")
        act_made = sem("act_made")
        out_stored = sem("out_stored")
        psum_full = sem("psum_full")
        slot_free = [sem(f"slot_free{s}") for s in range(2)]
        act_done = sem("act_done")
        dve_done = sem("dve_done")
        wr_zeroed = sem("wr_zeroed")
        wr_hi = sem("wr_hi")
        wr_lo = sem("wr_lo")
        proj_zeroed = sem("proj_zeroed")
        proj_landed = sem("proj_landed")

        def chunks(ap):
            return ap.rearrange("p (q c) -> p q c", c=CW)

        def cols(ps, rows_=128):
            return ps[:rows_, :].rearrange("p (q c) -> p q c", c=512)[:, :, :CW]

        def blocks(ps, n, w, rows_):
            return ps[:rows_, :n * 128].rearrange("p (j c) -> p j c", c=128)[:, :, :w]

        def v_cols(v):
            return v.rearrange("p j (h c) -> p j h c", c=64)[:, :, 0:4:3, :]

        def v_psum(ps):
            return ps[:T, :NT * 128].rearrange("p (j h c) -> p j h c", h=2, c=64)

        block = ctx.enter_context(nc.Block())

        @block.sync
        def _(sp):
            sp.dma_start(dsti[:, :], dst_cols).then_inc(edges_in, 16)
            sp.dma_start(srci[:, :], src_cols).then_inc(edges_in, 16)
            sp.dma_start(grp_i[:, :], dst_groups).then_inc(edges_in, 16)
            sp.dma_start(iota_t[:, :], iota).then_inc(edges_in, 16)
            sp.dma_start(gno[:, :], group_no[:, 0:2]).then_inc(edges_in, 16)
            sp.dma_start(tile_no[:, :], group_no[:, 2:2 + 2 * NT]).then_inc(edges_in, 16)
            sp.dma_start(ident[:, :], consts).then_inc(const_in, 16)
            sp.dma_start(rows[:, :], feat_rows).then_inc(const_in, 16)
            sp.dma_start(wr_raw[:, :], wr).then_inc(const_in, 16)
            for n in range(2):
                sp.dma_start(slab_raw[n][:, :], slabs[n]).then_inc(slab_landed[n], 16)

            def load_xs(layer, t):
                s = t % 2
                if layer == 1 and t == 0:
                    for r in range(2):
                        sp.wait_ge(x0_stored[r], 16 * NT // 2)
                if layer == 2 and t == 0:
                    sp.wait_ge(h_stored, 16 * KD)
                sp.dma_start(xs_raw[s][:, :, :].rearrange("p j c -> p (j c)"),
                             xs_d[layer - 1][t]).then_inc(xs_landed[s], 16)

            for k in ORDER:
                if k[0] == "LNA":
                    for i in range(NT):
                        if i >= 2:
                            sp.wait_ge(x_used, i - 1)
                        sp.dma_start(xt[i % 2][:, :], x[T * i:T * i + T, :]).then_inc(x_landed[i % 2], 16)
                elif k[0] == "LNB":
                    i = k[1]
                    sp.wait_ge(act_done, ACTED[k])
                    sp.dma_start(xn_d[T * i:T * i + T, :], xn[i % 2][:, :]).then_inc(xn_stored[i % 2], 16)
                    if i >= 2:
                        sp.wait_ge(x0_ready, i - 1)
                    sp.dma_start(pet[i % 2][:, :], pe[T * i:T * i + T, :]).then_inc(pe_landed[i % 2], 16)
                    sp.wait_ge(x0_ready, i + 1)
                    sp.dma_start(xs_d[0].rearrange("f p (j c) -> j p f c", c=128)[i],
                                 x0t[i % 2][:, :].rearrange("p (f c) -> p f c", c=128)
                                 ).then_inc(x0_stored[i % 2], 16)
                elif k[0] == "DEG":
                    load_xs(1, 0)
                    load_xs(1, 1)
                elif k[0] == "ZP":
                    _, layer, t = k
                    if layer == 2 and t == 0:
                        load_xs(2, 0)
                        load_xs(2, 1)
                    if t + 2 < KD:
                        sp.wait_ge(dve_done, DVED[k])
                        load_xs(layer, t + 2)
                elif k[0] == "P":
                    n = k[1]
                    if n + 2 < len(SLABS):
                        sp.wait_ge(dve_done, DVED[k])
                        sp.dma_start(slab_raw[n % 2][:, :], slabs[n + 2]).then_inc(slab_landed[n % 2], 16)
                elif k[0] == "HT":
                    sp.wait_ge(act_done, ACTED[k])
                    sp.dma_start(xs_d[1][k[1]], hout[:, :]).then_inc(h_stored, 16)
                elif k[0] == "H" and k[1] == 2:
                    f = k[2]
                    sp.wait_ge(act_done, ACTED[k])
                    sp.dma_start(gnn_d[f], htmp[f % 2][:, :]).then_inc(gnn_stored[f % 2], 16)
                    if f == 2:
                        for i in range(2):
                            sp.wait_ge(xn_stored[i], 16 * NT // 2)
                            sp.dma_start(xn_in[i][:, :], xn_d[T * i:T * i + T, :]).then_inc(xn_landed[i], 16)
                elif k[0] == "XT":
                    i = k[1]
                    if i + 2 < NT:
                        sp.wait_ge(psum_full, FULL[k])
                        sp.dma_start(xn_in[i % 2][:, :], xn_d[T * (i + 2):T * (i + 3), :]
                                     ).then_inc(xn_landed[i % 2], 16)
                elif k[0] == "MP":
                    sp.wait_ge(proj_zeroed, 1)
                    for h in range(2):
                        sp.dma_start(proj_raw[DH * h:DH * h + DH, FEAT * h:FEAT * h + FEAT], proj
                                     ).then_inc(proj_landed, 16)
                elif k[0] == "RC":
                    p = k[1]
                    sp.wait_ge(dve_done, DVED[k])
                    sp.dma_start(at_d[p], att[:, :]).then_inc(att_stored, 16)
                    if p == PAIRS - 1:
                        sp.wait_ge(att_stored, 16 * PAIRS)
                        for s in range(2):
                            sp.wait_ge(gnn_stored[s], 16 * KD // 2)
                            sp.dma_start(at_in[s][:, :], at_d[s]).then_inc(at_landed[s], 16)
                            sp.dma_start(gnn_in[s][:, :], gnn_d[s]).then_inc(gnn_landed[s], 16)
                            sp.dma_start(x_in[s][:, :, :],
                                         x.rearrange("(j p) (f c) -> f p j c", p=T, c=128)[s]
                                         ).then_inc(xr_landed[s], 16)
                elif k[0] == "AP":
                    if k[1] + 2 < KD:
                        sp.wait_ge(dve_done, DVED[k])
                        sp.dma_start(at_in[k[1] % 2][:, :], at_d[k[1] + 2]).then_inc(at_landed[k[1] % 2], 16)
                elif k[0] == "O":
                    f = k[1]
                    if f + 2 < KD:
                        sp.wait_ge(dve_done, DVED[k])
                        sp.dma_start(gnn_in[f % 2][:, :], gnn_d[f + 2]).then_inc(gnn_landed[f % 2], 16)
                elif k[0] == "OT":
                    f = k[1]
                    if f + 2 < KD:
                        sp.wait_ge(dve_done, DVED[k])
                        sp.dma_start(x_in[f % 2][:, :, :],
                                     x.rearrange("(j p) (f c) -> f p j c", p=T, c=128)[f + 2]
                                     ).then_inc(xr_landed[f % 2], 16)
                    if f == KD - 1:
                        sp.wait_ge(dve_done, DVED[k])
                        sp.dma_start(w2_raw[:, :, :].rearrange("p a c -> p (a c)"), w2[0]).then_inc(w2_landed, 16)
                        sp.dma_start(tie_t[:, :], tie).then_inc(const_in, 16)
                elif k[0] == "W2P":
                    e = k[1]
                    if e + 1 < EXP:
                        sp.wait_ge(dve_done, DVED[k])
                        sp.dma_start(w2_raw[:, :, :].rearrange("p a c -> p (a c)"), w2[e + 1]
                                     ).then_inc(w2_landed, 16)
                elif k[0] == "OUT" and k[1] == EXP - 1:
                    j = k[2]
                    sp.wait_ge(dve_done, DVED[k])
                    sp.dma_start(out[T * j:T * j + T, :], acc[:, j, :]).then_inc(out_stored, 16)
            sp.wait_ge(out_stored, 16 * NT)

        @block.gpsimd
        def _(pool):
            pool.memset(zeros[:, :], 0.0).then_inc(memset_done, 1)
            pool.memset(onesf[:, :], 1.0).then_inc(memset_done, 1)
            pool.memset(eps[:, :], LN_EPS).then_inc(memset_done, 1)
            pool.memset(adj[:, :, N:NP].bitcast(F32), 0.0).then_inc(memset_done, 1)
            pool.memset(dinv_b[:, N:NP], 0.0).then_inc(memset_done, 1)
            pool.memset(wr_p[0][:, :].bitcast(F32), 0.0)
            pool.memset(wr_p[1][:, :].bitcast(F32), 0.0).then_inc(wr_zeroed, 1)
            pool.wait_ge(keys_ready, 1)
            pool.partition_all_reduce(key_m[:, :], key_b[:, :], NG, bass.bass_isa.ReduceOp.max
                                      ).then_inc(keys_max, 1)
            for k in ORDER:
                if k[0] == "G":
                    b = k[1]
                    if b == 0:
                        pool.wait_ge(const_in, 16 * 3)
                    pool.wait_ge(act_done, ACTED[k])
                    blk = cnt[b % 2][:, T * b:T * b + T]
                    pool.tensor_tensor(blk, blk, ident[:T, :T], ALU.add).then_inc(diag_added, 1)
                elif k[0] == "MP":
                    pool.wait_ge(dve_done, DVED[("XT", 0)])
                    for s in range(2):
                        pool.wait_ge(gnn_stored[s], 16 * KD // 2)
                    for q in range(2):
                        pool.memset(v_p[q][:, :, 64:192].bitcast(F32), 1.0 - q)
                    pool.memset(proj_raw[:, :], 0.0).then_inc(proj_zeroed, 1)
                elif k[0] == "LNB":
                    i = k[1]
                    pool.wait_ge(act_done, ACTED[k])
                    pool.wait_ge(pe_landed[i % 2], 16 * (i // 2 + 1))
                    if i >= 2:
                        pool.wait_ge(x0_stored[i % 2], 16 * (i // 2))
                    pool.tensor_tensor(x0t[i % 2][:, :], xn[i % 2][:, :], pet[i % 2][:, :], ALU.add
                                       ).then_inc(x0_ready, 1)

        @block.scalar
        def _(act):
            links = [0]

            def link(ins):
                links[0] += 1
                ins.then_inc(achain, 1)
                act.wait_ge(achain, links[0])

            def done(k, ins, free=True):
                ins.then_inc(act_done, 1)

            copy = lambda o, i, **kw: act.activation(o, i, ACT.Copy, **kw)

            for k in ORDER:
                kind = k[0]
                if kind not in ACT_KINDS and kind not in ("LNA", "LNS", "DEG", "LN2"):
                    continue
                if kind in PSUM_KINDS:
                    u, s = FULL[k], slot_of(k)
                    ps = slot[s]
                    if kind not in ("Z", "VA"):
                        act.wait_ge(psum_full, u)
                if kind == "LNA":
                    for i in range(NT):
                        act.wait_ge(x_landed[i % 2], 16 * (i // 2 + 1))
                        link(act.activation(dx[:, i, :], xt[i % 2][:, :], ACT.Copy, accum_out=xsum[:, i:i + 1]))
                        link(copy(nmean[:, i:i + 1], xsum[:, i:i + 1], scale=-1.0 / D))
                        link(act.activation(dx[:, i, :], xt[i % 2][:, :], ACT.Identity, bias=nmean[:, i:i + 1]))
                        ins = act.activation(xt[i % 2][:, :], dx[:, i, :], ACT.Square, accum_out=vsum[:, i:i + 1])
                        ins.then_inc(x_used, 1)
                    act.wait_ge(x_used, NT)
                    act.wait_ge(memset_done, 5)
                    act.activation(std[:T, :], vsum[:, :], ACT.Sqrt, bias=eps[:T, :], scale=1.0 / D
                                   ).then_inc(ln_sums, 1)
                elif kind == "LNB":
                    i = k[1]
                    if i == 0:
                        act.wait_ge(rstd_ready, 1)
                    if i >= 2:
                        act.wait_ge(xn_stored[i % 2], 16 * (i // 2))
                        act.wait_ge(x0_ready, i - 1)
                    copy(xn[i % 2][:, :], dx[:, i, :], scale=rstd[:, i:i + 1]).then_inc(act_done, 1)
                elif kind == "G":
                    b = k[1]
                    copy(cnt[b % 2][:, 0:2 * CW].rearrange("p (q c) -> p q c", c=CW),
                         ps[:T, :1024].rearrange("p (q c) -> p q c", c=512)[:, :, :CW],
                         accum_out=degs[:, 2 * b:2 * b + 1])
                    ins = copy(cnt[b % 2][:, 2 * CW:N], ps[:T, 1024:1024 + N - 2 * CW],
                               accum_out=degs[:, 2 * b + 1:2 * b + 2])
                    ins.then_inc(act_done, 1)
                elif kind == "GT":
                    b = k[1]
                    copy(adj[:, :, T * b:T * b + T], blocks(ps, NT, T, T)).then_inc(act_done, 1)
                elif kind == "DEG":
                    act.wait_ge(dinv_ready, 1)
                    act.activation(std[:T, :], nw[:T, 0:NT], ACT.Sqrt).then_inc(deg_sqrt, 1)
                    act.wait_ge(const_in, 16 * 3)
                    act.wait_ge(wr_zeroed, 1)
                    for q in range(2):
                        copy(wr_p[q][:, 0:KD * 2 * EXP].rearrange("p (k e) -> p k e", e=2 * EXP)[:, :, 0:EXP],
                             wr_raw[:, :].rearrange("p (k e) -> p k e", e=EXP)).then_inc(wr_hi, 1)
                elif kind == "DB":
                    copy(dinv_b[:, 0:N].rearrange("p (j c) -> p j c", c=T), blocks(ps, NT, T, 128)
                         ).then_inc(act_done, 1)
                elif kind == "ZP":
                    _, layer, t = k
                    act.wait_ge(xs_scaled, (layer - 1) * KD + t + 1)
                    if t >= 2:
                        act.wait_ge(psum_full, FULL[("Z", layer, t - 2)])
                    copy(xs_p[t % 2][0][:, :, :], xs_raw[t % 2][:, :, :]).then_inc(act_done, 1)
                elif kind == "Z":
                    _, layer, t = k
                    act.wait_ge(z_scaled, (layer - 1) * KD + t + 1)
                    copy(big[0][:, t, :], ztmp[t % 2][:, :]).then_inc(act_done, 1)
                elif kind == "P":
                    n = k[1]
                    if n == 0:
                        act.wait_ge(wr_lo, 1)
                    act.wait_ge(slab_landed[n % 2], 16 * (n // 2 + 1))
                    if n >= 2:
                        act.wait_ge(psum_full, FULL[SLABS[n - 2]])
                    copy(slab_p[n % 2][0][:, :, :], slab_raw[n % 2][:, :].rearrange("p (k c) -> p k c", c=128)
                         ).then_inc(act_done, 1)
                elif kind == "H" and k[1] == 1:
                    f = k[2]
                    h = htmp[f % 2]
                    act.activation(chunks(h[:, :]), cols(ps), ACT.Identity, bias=b1c[:, f:f + 1]
                                   ).then_inc(h_biased, 1)
                    act.wait_ge(bn_ready, f + 1)
                    act.activation(std[:, 0:1], bmv[:, 1:2], ACT.Sqrt, bias=eps[:, :]).then_inc(std_ready, 1)
                    act.wait_ge(bn_affine, f + 1)
                    act.activation(h[:, :], h[:, :], ACT.Relu, bias=bsc[:, 1:2], scale=bsc[:, 0:1]
                                   ).then_inc(act_done, 1)
                elif kind == "H":
                    f = k[2]
                    if f >= 2:
                        act.wait_ge(gnn_stored[f % 2], 16 * (f // 2))
                    act.activation(chunks(htmp[f % 2][:, :]), cols(ps), ACT.Relu, bias=b2c[:, f:f + 1]
                                   ).then_inc(act_done, 1)
                elif kind == "HT":
                    if k[1]:
                        act.wait_ge(h_stored, 16 * k[1])
                    copy(hout[:, :], ps[:T, :NT * 128]).then_inc(act_done, 1)
                elif kind in ("XT", "FT"):
                    i = k[1]
                    copy(big[0][:, :, T * i:T * i + T], blocks(ps, KD, T, 128)).then_inc(act_done, 1)
                elif kind == "V":
                    copy(chunks(vt[:, :]), cols(ps)).then_inc(act_done, 1)
                elif kind == "VT":
                    copy(v_cols(v_p[0][:, :, :]), v_psum(ps)).then_inc(act_done, 1)
                elif kind in ("K", "Q"):
                    copy(chunks((k_p if kind == "K" else q_p)[0][:, :]), cols(ps)).then_inc(act_done, 1)
                elif kind == "KK":
                    act.activation(kk_p[k[2] % 2][0][:, :], ps[:T, :2 * FEAT], ACT.Relu).then_inc(act_done, 1)
                elif kind == "KC":
                    act.wait_ge(kv_full, k[1] + 1)
                    copy(kvt[:, :], kvb[:, :]).then_inc(act_done, 1)
                elif kind == "S":
                    copy(s_p[0][:, :, :, :].rearrange("p h f c -> p (h f c)"), ps[:, :512]).then_inc(act_done, 1)
                elif kind == "MP":
                    act.wait_ge(proj_landed, 32)
                    copy(proj_p[0][:, :], proj_raw[:, :]).then_inc(act_done, 1)
                elif kind == "QP":
                    act.activation(chunks(qp_p[0][:, k[3], :]), cols(ps), ACT.Relu).then_inc(act_done, 1)
                elif kind == "AT":
                    p, h = k[1], k[2]
                    if p == 0 and h == 0:
                        for s_ in range(2):
                            act.wait_ge(gnn_stored[s_], 16 * KD // 2)
                    if p and h == 0:
                        act.wait_ge(dve_done, DVED[("RC", p - 1)])
                    o, a, b = 64 * h, 64 * h, 64 - 64 * h
                    copy(chunks(num[o:o + 64, :]), cols(ps)[a:a + 64])
                    ins = copy(chunks(nrm[o:o + 64, :]), cols(ps)[b:b + 64], bias=ATT_EPS)
                    ins.then_inc(act_done, 1)
                elif kind == "AP":
                    t = k[1]
                    act.wait_ge(at_landed[t % 2], 16 * (t // 2 + 1))
                    copy(big[0][:, t, :], at_in[t % 2][:, :]).then_inc(act_done, 1)
                elif kind == "LN2":
                    act.wait_ge(ln2_var, 1)
                    act.activation(std[:T, :], l2mv[:, 1:2 * NT:2], ACT.Sqrt, bias=eps[:T, :]).then_inc(ln2_std, 1)
                elif kind == "R":
                    copy(chunks(lgt[:, :]), cols(ps, 2 * EXP)).then_inc(act_done, 1)
                elif kind == "RT":
                    copy(lg2[:, :], ps[:T, :NT * 2 * EXP]).then_inc(act_done, 1)
                    act.wait_ge(exp_in, 1)
                    act.activation(rsm[:, 3 * NT:4 * NT], rsm[:, 2 * NT:3 * NT], ACT.Exp).then_inc(exp_out, 1)
                elif kind == "W2P":
                    e = k[1]
                    act.wait_ge(w2_landed, 16 * (e + 1))
                    if e:
                        act.wait_ge(psum_full, FULL[("OUT", e - 1, NT - 1)])
                    copy(w2_p[0][:, :, :], w2_raw[:, :, :]).then_inc(act_done, 1)
                elif kind == "GA":
                    e, t = k[1], k[2]
                    if e == 0 and t == 0:
                        act.wait_ge(dve_done, DVED[("RT",)])
                    elif 2 * e + t:
                        act.wait_ge(act_made, 2 * e + t)
                    act.activation(chunks(sil[:, :]), cols(ps), ACT.Silu).then_inc(act_done, 1)
                elif kind == "VA":
                    e, t = k[1], k[2]
                    act.wait_ge(act_made, 2 * e + t + 1)
                    copy(a_p[0][:, t, :], actt[:, :]).then_inc(act_done, 1)

        @block.vector
        def _(dve):
            links = [0]

            def link(ins):
                links[0] += 1
                ins.then_inc(chain, 1)
                dve.wait_ge(chain, links[0])

            def tt(o, a, b, op):
                return dve.tensor_tensor(o, a, b, op)

            def ts(o, a, s1, op0, s2=None, op1=None):
                return dve.tensor_scalar(o, a, s1, s2, op0, op1) if op1 is not None else \
                    dve.tensor_scalar(o, a, s1, None, op0)

            def newton(res, v, root, n, rows_, tmp):
                a, b = tmp[:rows_, 0:n], tmp[:rows_, n:2 * n]
                link(dve.reciprocal(a, root))
                link(tt(b, a, a, ALU.mult))
                link(tt(b, b, v, ALU.mult))
                link(ts(b, b, -0.5, ALU.mult, 1.5, ALU.add))
                return tt(res, a, b, ALU.mult)

            def find_bounds():
                dve.wait_ge(edges_in, 16 * 6)
                dve.tensor_copy(dstf[:, :], dsti[:, :])
                dve.tensor_copy(srcf[:, :], srci[:, :])
                link(dve.tensor_copy(grp_f[:, :], grp_i[:, :]))
                dve.tensor_reduce(gmm[:, 0:1], grp_f[:, :], AX.X, ALU.min)
                link(dve.tensor_reduce(gmm[:, 1:2], grp_f[:, :], AX.X, ALU.max))
                link(ts(key_a[:, :], tile_no[:, 0:NT], gmm[:, 1:2], ALU.is_le))
                link(dve.scalar_tensor_tensor(out=key_a[:, :], in0=tile_no[:, NT:2 * NT], scalar=gmm[:, 0:1],
                                              in1=key_a[:, :], op0=ALU.is_gt, op1=ALU.mult))
                ts(key_b[:, 0:NT], key_a[:, :], gno[:, 1:2], ALU.mult)
                ts(key_b[:, NT:2 * NT], key_a[:, :], gno[:, 0:1], ALU.mult).then_inc(keys_ready, 1)
                dve.wait_ge(keys_max, 1)
                lo, hi, n_, st, w = (lims[0:1, NT * i:NT * i + NT] for i in range(5))
                link(ts(lo, key_m[0:1, 0:NT], -1.0, ALU.mult, float(NG), ALU.add))
                link(ts(lo, lo, float(NG - 1), ALU.min))
                link(ts(hi, lo, 1.0, ALU.add))
                link(tt(hi, hi, key_m[0:1, NT:2 * NT], ALU.max))
                link(tt(n_, hi, lo, ALU.subtract))
                cur, nxt = n_, st
                step = 1
                while step < NT:
                    dve.tensor_copy(nxt[:, 0:step], cur[:, 0:step])
                    link(tt(nxt[:, step:], cur[:, step:], cur[:, :NT - step], ALU.add))
                    cur, nxt = nxt, (w if nxt is st else st)
                    step *= 2
                link(tt(n_, hi, cur, ALU.subtract))
                dve.tensor_copy(bounds[:, 0:NT], cur)
                dve.tensor_copy(bounds[:, NT:2 * NT], n_).then_inc(bounds_ready, 1)

            find_bounds()
            dve.wait_ge(bounds_ready, 1)
            start = 0
            for k in ORDER:
                kind = k[0]
                if kind not in DVE_KINDS and kind not in ("G", "LNS", "DEG", "H", "LN2"):
                    continue
                if kind in PSUM_KINDS:
                    u, s = FULL[k], slot_of(k)
                    ps = slot[s]
                if kind == "G":
                    b = k[1]
                    end = dve.value_load(bounds[0:1, b:b + 1], min_val=1, max_val=NG * NT)
                    shift = dve.value_load(bounds[0:1, NT + b:NT + b + 1], min_val=-NG * NT, max_val=NG)
                    with dve.Fori(start, end) as r:
                        group = nc.s_assert_within(r + shift, 0, NG - 1, skip_runtime_bounds_check_because=
                                                   "find_bounds keeps every group within the edge list")
                        for j in range(GC):
                            c = group * GC + j
                            dve.wait_ge(oh_used[j], r + 1)
                            ts(oh_src[j][:, :], iota_t[:, :], srcf[:, bass.ds(c, 1)], ALU.is_equal)
                            ts(oh_dst[j][:, :], iota_t[:, T * b:T * b + T], dstf[:, bass.ds(c, 1)], ALU.is_equal
                               ).then_inc(oh_ready[j], 1)
                    start = end
                elif kind == "LNS":
                    dve.wait_ge(ln_sums, 1)
                    link(ts(nw[:T, 2 * NT:3 * NT], vsum[:, :], 1.0 / D, ALU.mult, LN_EPS, ALU.add))
                    newton(rstd[:, :], nw[:T, 2 * NT:3 * NT], std[:T, :], NT, T, nw[:, 3 * NT:]
                           ).then_inc(rstd_ready, 1)
                elif kind == "DEG":
                    dve.wait_ge(act_done, ACTED[("G", NT - 1)])
                    link(tt(nw[:T, 0:NT], degs[:, 0:2 * NT:2], degs[:, 1:2 * NT:2], ALU.add))
                    ts(nw[:T, 0:NT], nw[:T, 0:NT], 1.0, ALU.add).then_inc(dinv_ready, 1)
                    dve.wait_ge(deg_sqrt, 1)
                    link(newton(dinv[:, :], nw[:T, 0:NT], std[:T, :], NT, T, nw[:, NT:3 * NT]))
                    tt(diag[:, :, :], ident[:T, :T].unsqueeze(1).to_broadcast([T, NT, T]),
                       dinv[:, :].unsqueeze(2).to_broadcast([T, NT, T]), ALU.mult).then_inc(diag_ready, 1)
                    dve.wait_ge(wr_hi, 2)
                    w3 = wr_p[0][:, 0:KD * 2 * EXP].rearrange("p (k e) -> p k e", e=2 * EXP)
                    tt(w3[:, :, EXP:], wr_raw[:, :].rearrange("p (k e) -> p k e", e=EXP),
                       w3[:, :, 0:EXP].bitcast(F32), ALU.subtract).then_inc(wr_lo, 1)
                elif kind == "ZP":
                    _, layer, t = k
                    s_, n = t % 2, (layer - 1) * KD + t
                    dve.wait_ge(xs_landed[s_], 16 * (n // 2 + 1))
                    raw = xs_raw[s_][:, :, :]
                    tt(raw, raw, dinv[:, :].unsqueeze(2).to_broadcast([T, NT, 128]), ALU.mult
                       ).then_inc(xs_scaled, 1)
                    dve.wait_ge(act_done, ACTED[k])
                    tt(xs_p[s_][1][:, :, :], raw, xs_p[s_][0][:, :, :].bitcast(F32), ALU.subtract
                       ).then_inc(dve_done, 1)
                elif kind == "Z":
                    _, layer, t = k
                    dve.wait_ge(psum_full, u)
                    dve.wait_ge(act_done, ACTED[("DB",)])
                    tt(chunks(ztmp[t % 2][:, :]), cols(ps), chunks(dinv_b[:, :]), ALU.mult).then_inc(z_scaled, 1)
                    dve.wait_ge(act_done, ACTED[k])
                    tt(big[1][:, t, :], ztmp[t % 2][:, :], big[0][:, t, :].bitcast(F32), ALU.subtract
                       ).then_inc(dve_done, 1)
                elif kind == "P":
                    n = k[1]
                    dve.wait_ge(act_done, ACTED[k])
                    tt(slab_p[n % 2][1][:, :, :].rearrange("p k c -> p (k c)"), slab_raw[n % 2][:, :],
                       slab_p[n % 2][0][:, :, :].bitcast(F32).rearrange("p k c -> p (k c)"), ALU.subtract
                       ).then_inc(dve_done, 1)
                elif kind == "H":
                    if k[1] == 2:
                        continue
                    f = k[2]
                    h = htmp[f % 2]
                    dve.wait_ge(h_biased, f + 1)
                    for q in range(3):
                        a = q * CW
                        ins = dve.bn_stats(bst[:, 6 * q:6 * q + 6], h[:, a:min(a + CW, N)])
                    link(ins)
                    dve.bn_aggr(bmv[:, :], bst[:, :].rearrange("p (q c) -> p q c", c=6)).then_inc(bn_ready, 1)
                    dve.wait_ge(std_ready, f + 1)
                    link(ts(nw[:, 0:1], bmv[:, 1:2], BN_EPS, ALU.add))
                    link(newton(nw[:, 1:2], nw[:, 0:1], std[:, 0:1], 1, 128, nw[:, 2:4]))
                    link(tt(bsc[:, 0:1], nw[:, 1:2], gammac[:, f:f + 1], ALU.mult))
                    link(tt(nw[:, 4:5], bmv[:, 0:1], bsc[:, 0:1], ALU.mult))
                    tt(bsc[:, 1:2], betac[:, f:f + 1], nw[:, 4:5], ALU.subtract).then_inc(bn_affine, 1)
                elif kind in ("XT", "FT"):
                    i = k[1]
                    dve.wait_ge(act_done, ACTED[k])
                    tt(big[1][:, :, T * i:T * i + T], blocks(ps, KD, T, 128),
                       big[0][:, :, T * i:T * i + T].bitcast(F32), ALU.subtract).then_inc(dve_done, 1)
                elif kind == "VT":
                    dve.wait_ge(act_done, ACTED[k])
                    tt(v_cols(v_p[1][:, :, :]), v_psum(ps), v_cols(v_p[0][:, :, :].bitcast(F32)), ALU.subtract
                       ).then_inc(dve_done, 1)
                elif kind in ("K", "Q"):
                    parts = k_p if kind == "K" else q_p
                    dve.wait_ge(act_done, ACTED[k])
                    tt(chunks(parts[1][:, :]), cols(ps), chunks(parts[0][:, :].bitcast(F32)), ALU.subtract
                       ).then_inc(dve_done, 1)
                elif kind == "KK":
                    dve.wait_ge(act_done, ACTED[k])
                    dve.scalar_tensor_tensor(
                        out=kk_p[k[2] % 2][1][:, :], in0=ps[:T, :2 * FEAT], scalar=0.0,
                        in1=kk_p[k[2] % 2][0][:, :].bitcast(F32), op0=ALU.max, op1=ALU.subtract
                    ).then_inc(dve_done, 1)
                elif kind == "S":
                    dve.wait_ge(act_done, ACTED[k])
                    tt(s_p[1][:, :, :, :].rearrange("p h f c -> p (h f c)"), ps[:, :512],
                       s_p[0][:, :, :, :].bitcast(F32).rearrange("p h f c -> p (h f c)"), ALU.subtract
                       ).then_inc(dve_done, 1)
                elif kind == "MP":
                    dve.wait_ge(act_done, ACTED[k])
                    tt(proj_p[1][:, :], proj_raw[:, :], proj_p[0][:, :].bitcast(F32), ALU.subtract
                       ).then_inc(dve_done, 1)
                elif kind == "QP":
                    dve.wait_ge(act_done, ACTED[k])
                    dve.scalar_tensor_tensor(
                        out=chunks(qp_p[1][:, k[3], :]), in0=cols(ps), scalar=0.0,
                        in1=chunks(qp_p[0][:, k[3], :].bitcast(F32)), op0=ALU.max, op1=ALU.subtract
                    ).then_inc(dve_done, 1)
                elif kind == "RC":
                    p = k[1]
                    dve.wait_ge(act_done, ACTED[("AT", p, 1)])
                    link(dve.reciprocal(nrm[:, :], nrm[:, :]))
                    if p:
                        dve.wait_ge(att_stored, 16 * p)
                    tt(att[:, :], num[:, :], nrm[:, :], ALU.mult).then_inc(dve_done, 1)
                elif kind == "AP":
                    t = k[1]
                    dve.wait_ge(act_done, ACTED[k])
                    tt(big[1][:, t, :], at_in[t % 2][:, :], big[0][:, t, :].bitcast(F32), ALU.subtract
                       ).then_inc(dve_done, 1)
                elif kind == "O":
                    f = k[1]
                    dve.wait_ge(psum_full, u)
                    dve.wait_ge(gnn_landed[f % 2], 16 * (f // 2 + 1))
                    dve.scalar_tensor_tensor(out=chunks(otmp[f % 2][:, :]), in0=cols(ps), scalar=boc[:, f:f + 1],
                                             in1=chunks(gnn_in[f % 2][:, :]), op0=ALU.add, op1=ALU.add
                                             ).then_inc(dve_done, 1)
                elif kind == "OT":
                    f = k[1]
                    dve.wait_ge(psum_full, u)
                    dve.wait_ge(xr_landed[f % 2], 16 * (f // 2 + 1))
                    tt(acc[:, :, 128 * f:128 * f + 128], blocks(ps, NT, 128, T), x_in[f % 2][:, :, :], ALU.add
                       ).then_inc(dve_done, 1)
                elif kind == "LN2":
                    dve.wait_ge(dve_done, DVED[("OT", KD - 1)])
                    for j in range(NT):
                        dve.bn_stats(l2st[:, 0:6], acc[:, j, 0:512])
                        link(dve.bn_stats(l2st[:, 6:12], acc[:, j, 512:1024]))
                        link(dve.bn_aggr(l2mv[:, 2 * j:2 * j + 2], l2st[:, :].rearrange("p (q c) -> p q c", c=6)))
                    ts(nw[:T, 0:NT], l2mv[:, 1:2 * NT:2], LN_EPS, ALU.add).then_inc(ln2_var, 1)
                    dve.wait_ge(ln2_std, 1)
                    dve.wait_ge(ln2_var, 1)
                    link(newton(rstd[:, :], nw[:T, 0:NT], std[:T, :], NT, T, nw[:, NT:3 * NT]))
                elif kind == "FL":
                    j = k[1]
                    if j >= 2:
                        dve.wait_ge(psum_full, FULL[("FT", j - 2)])
                    ts(flat[j % 2][:, :], acc[:, j, :], l2mv[:, 2 * j:2 * j + 1], ALU.subtract,
                       rstd[:, j:j + 1], ALU.mult).then_inc(dve_done, 1)
                elif kind == "RT":
                    dve.wait_ge(act_done, ACTED[k])
                    dve.wait_ge(const_in, 16 * 4)
                    l_, rk, rt = lg[:, :, :], rank[:, :, :], rtmp[:, :, :]
                    two = lg2[:, :].rearrange("p (j e) -> p j e", e=2 * EXP)
                    link(tt(l_, two[:, :, 0:EXP], two[:, :, EXP:], ALU.add))
                    sh = [T, NT, EXP, EXP]
                    g4 = cmp_gt[:, :, :].rearrange("p j (e o) -> p j e o", o=EXP)
                    h4 = cmp_ge[:, :, :].rearrange("p j (e o) -> p j e o", o=EXP)
                    me, other = l_.unsqueeze(3).to_broadcast(sh), l_.unsqueeze(2).to_broadcast(sh)
                    tt(g4, other, me, ALU.is_gt)
                    link(tt(h4, other, me, ALU.is_equal))
                    link(tt(cmp_ge[:, :, :], cmp_ge[:, :, :],
                            tie_t[:, :].unsqueeze(1).to_broadcast([T, NT, EXP * EXP]), ALU.mult))
                    link(tt(cmp_gt[:, :, :], cmp_gt[:, :, :], cmp_ge[:, :, :], ALU.add))
                    link(dve.tensor_reduce(rk, g4, AX.X, ALU.add))
                    m1, m2, df, ex, w1, w2_ = (rsm[:, NT * i:NT * i + NT] for i in range(6))
                    dve.tensor_reduce(m1, l_, AX.X, ALU.max)
                    link(ts(rt, rk, 1.0, ALU.is_equal))
                    link(tt(rt, rt, l_, ALU.mult))
                    link(dve.tensor_reduce(m2, rt, AX.X, ALU.add))
                    tt(df, m2, m1, ALU.subtract).then_inc(exp_in, 1)
                    dve.wait_ge(exp_out, 1)
                    link(ts(w2_, ex, 1.0, ALU.add))
                    link(dve.reciprocal(w1, w2_))
                    link(tt(w2_, ex, w1, ALU.mult))
                    bc = lambda a: a.unsqueeze(2).to_broadcast([T, NT, EXP])
                    rw3 = rw[:, :].rearrange("p (j e) -> p j e", e=EXP)
                    ts(rt, rk, 1.0, ALU.is_equal)
                    link(ts(rw3, rk, 0.0, ALU.is_equal))
                    tt(rt, rt, bc(w2_), ALU.mult)
                    link(tt(rw3, rw3, bc(w1), ALU.mult))
                    tt(rw3, rw3, rt, ALU.add).then_inc(dve_done, 1)
                elif kind == "W2P":
                    dve.wait_ge(act_done, ACTED[k])
                    tt(w2_p[1][:, :, :], w2_raw[:, :, :], w2_p[0][:, :, :].bitcast(F32), ALU.subtract
                       ).then_inc(dve_done, 1)
                elif kind == "VA":
                    e, t = k[1], k[2]
                    dve.wait_ge(psum_full, u)
                    dve.wait_ge(act_done, ACTED[("GA", e, t)])
                    tt(chunks(actt[:, :]), cols(ps), chunks(sil[:, :]), ALU.mult).then_inc(act_made, 1)
                    dve.wait_ge(act_done, ACTED[k])
                    tt(a_p[1][:, t, :], actt[:, :], a_p[0][:, t, :].bitcast(F32), ALU.subtract
                       ).then_inc(dve_done, 1)
                elif kind == "OUT":
                    e, j = k[1], k[2]
                    dve.wait_ge(psum_full, u)
                    if e:
                        dve.wait_ge(dve_done, DVED[("OUT", e - 1, j)])
                    else:
                        dve.wait_ge(dve_done, DVED[("RT",)])
                    dve.scalar_tensor_tensor(out=acc[:, j, :], in0=ps[:T, :D],
                                             scalar=rw[:, j * EXP + e:j * EXP + e + 1],
                                             in1=acc[:, j, :], op0=ALU.mult, op1=ALU.add).then_inc(dve_done, 1)

        @block.tensor
        def _(ten):
            def free_slot(k):
                u = FULL[k] - 1
                if u >= 2:
                    before = UNITS[u - 2]
                    if before[0] in LAST_READER_DVE:
                        if before[0] == "Z":
                            ten.wait_ge(z_scaled, (before[1] - 1) * KD + before[2] + 1)
                        elif before[0] == "VA":
                            ten.wait_ge(act_made, 2 * before[1] + before[2] + 1)
                        else:
                            ten.wait_ge(dve_done, DVED[before])
                    else:
                        ten.wait_ge(act_done, ACTED[before])

            def slab_product(k, ps):
                n = SLAB[k]
                ten.wait_ge(dve_done, DVED[("P", n)])
                w = slab_p[n % 2]
                for kt in range(KD):
                    if k[0] == "O" and k[1] == 0:
                        ten.wait_ge(dve_done, DVED[("AP", kt)])
                    for c, (a, b) in enumerate(COMBOS):
                        for q in range(3):
                            mm = ten.matmul(ps[:, 512 * q:512 * q + CW], w[a][:, kt, :],
                                            big[b][:, kt, CW * q:CW * q + CW],
                                            start=(kt == 0 and c == 0), stop=(kt == KD - 1 and c == 2))
                return mm

            start = 0
            for k in ORDER:
                kind = k[0]
                if kind not in PSUM_KINDS and kind != "KV":
                    continue
                if kind in PSUM_KINDS:
                    ps = slot[slot_of(k)]
                    free_slot(k)
                if kind == "G":
                    b = k[1]
                    if b == 0:
                        ten.wait_ge(memset_done, 5)
                        ten.wait_ge(bounds_ready, 1)
                        for j in range(GC):
                            ten.sem_inc(oh_used[j], 1)
                    end = ten.value_load(bounds[0:1, b:b + 1], min_val=1, max_val=NG * NT)
                    span = [(512 * q, CW * q, min(CW, N - CW * q)) for q in range(3)]
                    for to, at_, w in span:
                        ten.matmul(ps[:T, to:to + w], zeros[:T, :T], iota_t[:, at_:at_ + w],
                                   start=True, stop=False, skip_group_check=True)
                    with ten.Fori(start, end) as r:
                        for j in range(GC):
                            ten.wait_ge(oh_ready[j], r + 1)
                            for q, (to, at_, w) in enumerate(span):
                                mm = ten.matmul(ps[:T, to:to + w], oh_dst[j][:, :], oh_src[j][:, at_:at_ + w],
                                                start=False, stop=False, skip_group_check=True)
                            mm.then_inc(oh_used[j], 1)
                    for to, at_, w in span:
                        mm = ten.matmul(ps[:T, to:to + w], zeros[:T, :T], iota_t[:, at_:at_ + w],
                                        start=False, stop=True, skip_group_check=True)
                    start = end
                elif kind == "GT":
                    b = k[1]
                    ten.wait_ge(diag_added, b + 1)
                    for j in range(NT):
                        mm = ten.transpose(ps[:T, 128 * j:128 * j + T], cnt[b % 2][:, T * j:T * j + T],
                                           ident[:T, :T])
                elif kind == "DB":
                    ten.wait_ge(diag_ready, 1)
                    for j in range(NT):
                        mm = ten.matmul(ps[:, 128 * j:128 * j + T], onesf[:T, :], diag[:, j, :],
                                        start=True, stop=True)
                elif kind == "Z":
                    _, layer, t = k
                    ten.wait_ge(dve_done, DVED[("ZP", layer, t)])
                    for j in range(NT):
                        for a in range(2):
                            for q in range(3):
                                mm = ten.matmul(ps[:, 512 * q:512 * q + CW], xs_p[t % 2][a][:, j, :],
                                                adj[:, j, CW * q:CW * q + CW],
                                                start=(j == 0 and a == 0), stop=(j == NT - 1 and a == 1))
                elif kind in ("H", "V", "K", "Q", "O", "GA", "VA"):
                    if kind == "H" and k[2] == 0:
                        ten.wait_ge(dve_done, DVED[("Z", k[1], KD - 1)])
                    if kind == "Q" and k[1] == 0:
                        ten.wait_ge(dve_done, DVED[("MP",)])
                    if kind == "V" and k[1] == 0:
                        ten.wait_ge(dve_done, DVED[("XT", NT - 1)])
                    if kind == "GA" and k[1] == 0 and k[2] == 0:
                        ten.wait_ge(dve_done, DVED[("FT", NT - 1)])
                    mm = slab_product(k, ps)
                elif kind in ("HT", "VT", "OT"):
                    if kind == "HT":
                        src_t = htmp[k[1] % 2]
                        ten.wait_ge(act_done, ACTED[("H", 1, k[1])])
                    elif kind == "VT":
                        src_t = vt
                        ten.wait_ge(act_done, ACTED[("V", k[1])])
                    else:
                        src_t = otmp[k[1] % 2]
                        ten.wait_ge(dve_done, DVED[("O", k[1])])
                    for j in range(NT):
                        mm = ten.transpose(ps[:T, 128 * j:128 * j + 128], src_t[:, T * j:T * j + T], ident[:, :])
                elif kind in ("XT", "FT"):
                    i = k[1]
                    if kind == "XT":
                        src_t = xn_in[i % 2]
                        ten.wait_ge(xn_landed[i % 2], 16 * (i // 2 + 1))
                    else:
                        src_t = flat[i % 2]
                        ten.wait_ge(dve_done, DVED[("FL", i)])
                    for j in range(KD):
                        mm = ten.transpose(ps[:, 128 * j:128 * j + T], src_t[:, 128 * j:128 * j + 128],
                                           ident[:T, :T])
                elif kind == "KK":
                    p, i = k[1], k[2]
                    if i == 0:
                        ten.wait_ge(dve_done, DVED[("K", p)])
                    for c, (a, b) in enumerate(COMBOS):
                        mm = ten.matmul(ps[:T, :2 * FEAT], k_p[a][:, T * i:T * i + T], proj_p[b][:, :],
                                        start=(c == 0), stop=(c == 2))
                elif kind == "KV":
                    p, i = k[1], k[2]
                    ten.wait_ge(dve_done, DVED[("KK", p, i)])
                    if i == 0:
                        ten.wait_ge(dve_done, DVED[("VT", p)])
                        if p:
                            ten.wait_ge(act_done, ACTED[("KC", p - 1)])
                    for h in range(2):
                        for c, (a, b) in enumerate(COMBOS):
                            mm = ten.matmul(kvb[:, FEAT * h:FEAT * h + FEAT], v_p[a][:, i, 128 * h:128 * h + 128],
                                            kk_p[i % 2][b][:, FEAT * h:FEAT * h + FEAT],
                                            start=(i == 0 and h == 0 and c == 0), stop=(i == NT - 1),
                                            skip_group_check=True)
                    if i == NT - 1:
                        mm.then_inc(kv_full, 1)
                    continue
                elif kind == "S":
                    ten.wait_ge(act_done, ACTED[("KC", k[1])])
                    for q in range(4):
                        mm = ten.transpose(ps[:, 128 * q:128 * q + 128], kvt[:, 128 * q:128 * q + 128], ident[:, :])
                elif kind == "QP":
                    p, h, f = k[1:]
                    if h == 0 and f == 0:
                        ten.wait_ge(dve_done, DVED[("Q", p)])
                    o = FEAT * h + 128 * f
                    for c, (a, b) in enumerate(COMBOS):
                        for q in range(3):
                            mm = ten.matmul(ps[:, 512 * q:512 * q + CW], proj_p[a][:, o:o + 128],
                                            q_p[b][:, CW * q:CW * q + CW], start=(c == 0), stop=(c == 2))
                elif kind == "AT":
                    p, h = k[1], k[2]
                    ten.wait_ge(dve_done, DVED[("S", p)])
                    ten.wait_ge(dve_done, DVED[("QP", p, h, 1)])
                    for f in range(2):
                        for c, (a, b) in enumerate(COMBOS):
                            for q in range(3):
                                mm = ten.matmul(ps[:, 512 * q:512 * q + CW], s_p[a][:, h, f, :],
                                                qp_p[b][:, f, CW * q:CW * q + CW],
                                                start=(f == 0 and c == 0), stop=(f == 1 and c == 2))
                elif kind == "R":
                    ten.wait_ge(dve_done, DVED[("FT", NT - 1)])
                    for kt in range(KD):
                        for a in range(2):
                            for q in range(3):
                                mm = ten.matmul(ps[:, 512 * q:512 * q + CW],
                                                wr_p[a][:, 2 * EXP * kt:2 * EXP * kt + 128],
                                                big[a][:, kt, CW * q:CW * q + CW],
                                                start=(kt == 0 and a == 0), stop=(kt == KD - 1 and a == 1))
                elif kind == "RT":
                    ten.wait_ge(act_done, ACTED[("R",)])
                    for j in range(NT):
                        mm = ten.transpose(ps[:T, 2 * EXP * j:2 * EXP * j + 2 * EXP], lgt[:, T * j:T * j + T],
                                           ident[:2 * EXP, :2 * EXP])
                elif kind == "OUT":
                    e, j = k[1], k[2]
                    if j == 0:
                        ten.wait_ge(dve_done, DVED[("VA", e, 1)])
                        ten.wait_ge(dve_done, DVED[("W2P", e)])
                    for f in range(2):
                        for c, (a, b) in enumerate(COMBOS):
                            for q in range(2):
                                mm = ten.matmul(ps[:T, 512 * q:512 * q + 512], a_p[a][:, f, T * j:T * j + T],
                                                w2_p[b][:, f, 512 * q:512 * q + 512],
                                                start=(f == 0 and c == 0), stop=(f == 1 and c == 2))
                mm.then_inc(psum_full, 1)


UNITS = [k for k in ORDER if k[0] in PSUM_KINDS]
LAST_READER_DVE = {"Z", "XT", "FT", "VT", "K", "Q", "KK", "QP", "S", "O", "OT", "VA", "OUT"}


def encoding():
    pos = np.arange(N, dtype=np.float32)[:, None]
    div = np.exp(np.arange(0, D, 2, dtype=np.float32) * np.float32(-np.log(10000.0) / D)).astype(np.float32)
    ang = (pos * div).astype(np.float32)
    return np.stack([np.sin(ang), np.cos(ang)], axis=-1).reshape(N, D).astype(np.float32)


def kernel(x, src, dst, L0_gnn_W1, L0_gnn_b1, L0_gnn_gamma, L0_gnn_beta, L0_gnn_W2, L0_gnn_b2,
           L0_mix_Wq, L0_mix_Wk, L0_mix_Wv, L0_mix_proj, L0_mix_Wo, L0_mix_bo,
           L0_ffn_Wr, L0_ffn_W1, L0_ffn_W2):
    from concourse import bacc
    from concourse.bass_utils import run_bass_kernel_spmd

    def columns(w):
        return np.asarray(w).reshape(KD, 128, KD, 128).transpose(2, 1, 0, 3).reshape(KD, 128, D)

    by_name = {("H", 1): columns(L0_gnn_W1), ("H", 2): columns(L0_gnn_W2), "V": columns(L0_mix_Wv),
               "K": columns(L0_mix_Wk), "Q": columns(L0_mix_Wq), "O": columns(L0_mix_Wo)}
    w1 = np.asarray(L0_ffn_W1).reshape(EXP, 2, 2, 128, KD, 128).transpose(0, 1, 2, 5, 4, 3)
    w1 = w1.reshape(EXP, 2, 2, 128, D)

    def slab(key):
        if key[0] in ("GA", "VA"):
            return w1[key[1], int(key[0] == "GA"), key[2]]
        return by_name[key[:2] if key[0] == "H" else key[0]][key[-1]]

    f = np.asarray
    as_cols = lambda v: f(v).reshape(KD, 128).T
    arrays = {
        "x": f(x),
        "src_cols": f(src).reshape(NCH, CH).T, "dst_cols": f(dst).reshape(NCH, CH).T,
        "dst_groups": f(dst).reshape(NG, GC * CH),
        "slabs": np.stack([slab(k) for k in SLABS]),
        "w2": f(L0_ffn_W2).reshape(EXP, D, 2, 128).transpose(0, 3, 2, 1).reshape(EXP, 128, 2 * D),
        "wr": f(L0_ffn_Wr).reshape(EXP, KD, 128).transpose(2, 1, 0).reshape(128, KD * EXP),
        "proj": f(L0_mix_proj),
        "feat_rows": np.concatenate([as_cols(v) for v in (L0_gnn_b1, L0_gnn_gamma, L0_gnn_beta, L0_gnn_b2,
                                                          L0_mix_bo)], axis=1),
        "consts": np.eye(128, dtype=np.float32),
        "group_no": np.concatenate([
            np.stack([np.arange(NG) + 1, NG - np.arange(NG)], axis=1),
            np.tile(np.arange(NT) * T, (NG, 1)), np.tile(np.arange(NT) * T + T, (NG, 1))], axis=1
        ).astype(np.float32),
        "tie": np.tile(np.tril(np.ones((EXP, EXP), np.float32), -1).reshape(1, -1), (T, 1)),
        "iota": np.tile(np.arange(N, dtype=np.float16)[None], (T, 1)),
        "pe": encoding(),
    }
    arrays = {k: np.ascontiguousarray(v) for k, v in arrays.items()}
    nc = bacc.Bacc("TRN2", target_bir_lowering=False, num_devices=1)
    args = {k: nc.dram_tensor(k + "_dram", v.shape, mybir.dt.from_np(v.dtype), kind="ExternalInput").ap()
            for k, v in arrays.items()}
    out = nc.dram_tensor("out_dram", (N, D), F32, kind="ExternalOutput").ap()
    build(nc, **args, out=out)
    r = run_bass_kernel_spmd(nc, [{k + "_dram": v for k, v in arrays.items()}], core_ids=[0])
    return r.results[0]["out_dram"]
```

```python
from contextlib import ExitStack

import numpy as np

import concourse.bass as bass
from concourse import mybir


F32 = mybir.dt.float32
F32R = mybir.dt.float32r
BF16 = mybir.dt.bfloat16
F16 = mybir.dt.float16
I32 = mybir.dt.int32
U32 = mybir.dt.uint32
ALU = mybir.AluOpType
ACT = mybir.ActivationFunctionType
AX = mybir.AxisListType

N, D = 1250, 1024
T = 125
NT = N // T
KD = D // 128
CW = 418
NP = 3 * CW
NE = 40000
CH = 125
NCH = NE // CH
GC = 4
NG = NCH // GC
HEADS, DH, FEAT = 16, 64, 256
PAIRS = HEADS // 2
EXP, FF = 8, 256
BN_EPS, LN_EPS, ATT_EPS = 1e-5, 1e-5, 1e-8
COMBOS = ((0, 0), (0, 1), (1, 0))


def slab_steps():
    s = [("H", 1, f) for f in range(KD)] + [("H", 2, f) for f in range(KD)]
    s += [("V", 0), ("K", 0), ("Q", 0)]
    for p in range(1, PAIRS):
        s += [("K", p), ("Q", p), ("V", p)]
    s += [("O", f) for f in range(KD)]
    return s


SLABS = slab_steps()
SLAB = {k: n for n, k in enumerate(SLABS)}


def steps():
    o = [("LNA",)]
    for b in range(NT):
        o.append(("G", b))
        if b == 3:
            o.append(("LNS",))
            o += [("LNB", i) for i in range(2)]
        if 4 <= b < 8:
            o += [("LNB", i) for i in range(2 * b - 6, 2 * b - 4)]
        if b:
            o.append(("GT", b - 1))
    o += [("GT", NT - 1), ("DEG",), ("DB",)]

    def with_split(key):
        n = SLAB[key] + 1
        return ([("P", n)] if n < len(SLABS) else []) + [key]

    o += [("ZP", 1, 0)]
    for layer in (1, 2):
        for t in range(KD):
            if t + 1 < KD:
                o.append(("ZP", layer, t + 1))
            if t == KD - 1 and layer == 1:
                o.append(("P", 0))
            o.append(("Z", layer, t))
            if layer == 2 and t == 0:
                o.append(("HT", KD - 1))
        for f in range(KD):
            if layer == 1 and f == KD - 1:
                o.append(("ZP", 2, 0))
            o += with_split(("H", layer, f))
            if layer == 1 and f:
                o.append(("HT", f - 1))
    o += [("XT", i) for i in range(NT)] + [("MP",)]
    o += with_split(("V", 0)) + with_split(("K", 0)) + [("VT", 0)] + with_split(("Q", 0))
    for p in range(PAIRS):
        more = p + 1 < PAIRS
        o += ([("KK", p, 0)] if p == 0 else []) + [("KK", p, 1), ("KK", p, 2)]
        for i in range(3, NT):
            o += [("KV", p, i - 3), ("KK", p, i)]
        o += [("KV", p, NT - 3), ("KV", p, NT - 2), ("QP", p, 0, 0), ("KV", p, NT - 1), ("KC", p),
              ("QP", p, 0, 1), ("S", p)]
        o += with_split(("K", p + 1)) if more else []
        o += [("AT", p, 0), ("QP", p, 1, 0), ("QP", p, 1, 1)]
        o += with_split(("Q", p + 1)) if more else []
        o += [("AT", p, 1), ("RC", p)]
        o += with_split(("V", p + 1)) + [("KK", p + 1, 0), ("RH", p), ("VT", p + 1)] if more else [("RH", p)]
    for f in range(KD):
        o += with_split(("O", f))
        if f:
            o.append(("OT", f - 1))
    o += [("OT", KD - 1), ("LN2",), ("FL", 0)]
    for j in range(NT):
        if j + 1 < NT:
            o.append(("FL", j + 1))
        o.append(("FT", j))
    o += [("R",), ("RT",), ("PX",)]
    return o


ORDER = steps()
PSUM_KINDS = {"G", "GT", "DB", "Z", "H", "HT", "XT", "V", "VT", "K", "Q", "KK", "QP", "AT",
              "O", "OT", "FT", "R", "RT", "PX"}
ACT_KINDS = PSUM_KINDS - {"O", "OT", "PX"} | {"P", "ZP", "KC", "S", "RH", "LNB", "MP"}
DVE_KINDS = {"ZP", "Z", "P", "XT", "VT", "K", "Q", "KK", "S", "QP", "RC", "RH", "O", "OT",
             "FL", "FT", "RT", "PX", "MP"}


def numbered(kinds, order=ORDER):
    return {k: n + 1 for n, k in enumerate(k for k in order if k[0] in kinds)}


FULL = numbered(PSUM_KINDS)
ACTED = numbered(ACT_KINDS)
DVED = numbered(DVE_KINDS)


def slot_of(key):
    return (FULL[key] - 1) % 2


RT_ = 105
NRT = 4
CAP = NRT * RT_
ROUNDS = -(-N // CAP)
HALVES = FF // 128
WS = 2 * HALVES
NWS = EXP * WS


def round_steps():
    o = [("LD", 0), ("LS", 0), ("LD", 1), ("WP", 0), ("LS", 1), ("WP", 1)]
    o += [("XE", 0, i) for i in range(NRT)] + [("W2P", 0)]
    for e in range(EXP):
        for n, key in enumerate((("GA", e, 0), ("VA", e, 0), ("GA", e, 1), ("VA", e, 1))):
            m = WS * e + n + 2
            o += [("WP", m)] if m < NWS else []
            o.append(key)
            if e + 2 < EXP and n == 0:
                o.append(("LD", e + 2))
            if e + 1 < EXP and n >= 1:
                o.append(("XE", e + 1, n - 1))
            if e + 1 < EXP and n == 1:
                o.append(("W2P", e + 1))
        o += [("LS", e + 2)] if e + 2 < EXP else []
        if e + 1 < EXP:
            o.append(("XE", e + 1, NRT - 1))
        o += [("OUT", e, i) for i in range(NRT)]
    return o


ROUND = round_steps()
WIDE = numbered({"XE", "OUT"}, ROUND)
NARROW = numbered({"GA", "VA"}, ROUND)
R_FULL = numbered({"XE", "OUT", "GA", "VA", "LS"}, ROUND)
R_ACT = numbered({"WP", "W2P", "XE", "GA", "VA", "OUT"}, ROUND)
R_DVE = numbered({"WP", "W2P", "XE", "VA", "LS"}, ROUND)
WIDE_KEYS, NARROW_KEYS = list(WIDE), list(NARROW)


def build(nc, x, src_cols, dst_cols, dst_groups, slabs, w1, w2, wr, proj, feat_rows, consts, group_no, tie,
          iota, pe, blank, before, places, tokens, out):
    ctx = ExitStack()
    with ctx:
        sem = lambda name: ctx.enter_context(nc.semaphore(name))
        small = lambda name, shape, dt=F32: ctx.enter_context(nc.sbuf_tensor(name, shape, dt))

        ident = small("ident", [128, 128])
        onesf = small("onesf", [128, 128])
        zeros = small("zeros", [128, 128], BF16)
        eps = small("eps", [128, 1])
        rows = small("rows", [128, 5 * KD])
        b1c, gammac, betac, b2c, boc = (rows[:, KD * i:KD * i + KD] for i in range(5))
        wr_p = [small(f"wr_{n}", [128, (KD - 1) * 2 * EXP + 128], F32R) for n in ("hilo", "hi0")]
        gno = small("gno", [NG, 2])
        tile_no = small("tile_no", [NG, 2 * NT])
        gmm = small("gmm", [NG, 2])
        key_a = small("key_a", [NG, NT])
        key_b = small("key_b", [NG, 2 * NT])
        key_m = small("key_m", [NG, 2 * NT])
        lims = small("lims", [1, 6 * NT])
        bounds = small("bounds", [1, 3 * NT], I32)
        degs = small("degs", [T, 2 * NT])
        dinv = small("dinv", [T, NT])
        nw = small("nw", [128, 6 * NT])
        xsum = small("xsum", [T, NT])
        nmean = small("nmean", [T, NT])
        vsum = small("vsum", [T, NT])
        std = small("std", [128, NT])
        rstd = small("rstd", [T, NT])
        bst = small("bst", [128, 3 * 6])
        bmv = small("bmv", [128, 2])
        bsc = small("bsc", [128, 2])
        l2mv = small("l2mv", [T, 2 * NT])
        rw = small("rw", [T, NT * EXP])
        place_no = small("place_no", [RT_, NRT])
        token = [small(f"token{s}", [RT_, NRT], U32) for s in range(4)]
        share = [small(f"share{s}", [RT_, NRT]) for s in range(4)]
        ls_a = small("ls_a", [RT_, NRT])
        ls_b = small("ls_b", [RT_, NRT])
        rounds_n = small("rounds_n", [1, 1], I32)

        base = (nc.sbuf_base + 31) // 32 * 32

        def at(name, off, shape, dt=F32):
            return nc.alloc_sbuf_tensor_at(name, shape, dt, offset=base + off)

        BIG = 2 * KD * NP * 4
        big = [at("big_hi", 0, [128, KD, NP], F32R), at("big_lo", BIG // 2, [128, KD, NP], F32R)]
        slab_raw = [at(f"slab_raw{s}", BIG + 4096 * s, [128, KD * 128]) for s in range(2)]
        slab_p = [[at(f"slab_{'hl'[q]}{s}", BIG + 8192 + 8192 * s + 4096 * q, [128, KD, 128], F32R)
                   for q in range(2)] for s in range(2)]
        R = BIG + 24576
        wr_raw = at("wr_raw", BIG + 8192 + 12288, [128, KD * EXP])
        dx = at("dx", 0, [T, NT, D])
        xt = [at(f"xt{s}", 40960 + 4096 * s, [T, D]) for s in range(2)]
        xn = [at(f"xn{s}", 49152 + 4096 * s, [T, D]) for s in range(2)]
        grp_i = at("grp_i", 49152, [NG, GC * CH], I32)
        grp_f = at("grp_f", 51168, [NG, GC * CH])
        iota_t = at("iota_t", 57344, [T, N], F16)
        oh_src = [at(f"oh_src{j}", 59872 + 2528 * j, [T, N], BF16) for j in range(GC)]
        oh_dst = [at(f"oh_dst{j}", 69984 + 256 * j, [T, T], BF16) for j in range(GC)]
        srcf = at("srcf", 71008, [CH, NCH])
        dstf = at("dstf", 72288, [CH, NCH])
        srci = at("srci", 73568, [CH, NCH], I32)
        dsti = at("dsti", 74848, [CH, NCH], I32)
        adj = at("adj", R, [T, NT, NP], F32R)
        XS = R + 50176
        xs_raw = [at(f"xs_raw{s}", XS + 5120 * s, [T, NT, 128]) for s in range(2)]
        xs_p = [[at(f"xs_{'hl'[q]}{s}", XS + 10240 + 10240 * s + 5120 * q, [T, NT, 128], F32R)
                 for q in range(2)] for s in range(2)]
        pet = [at(f"pet{s}", XS + 4096 * s, [T, D]) for s in range(2)]
        x0t = [at(f"x0t{s}", XS + 8192 + 4096 * s, [T, D]) for s in range(2)]
        ZT = XS + 30720
        ztmp = [at(f"ztmp{s}", ZT + 5024 * s, [128, NP]) for s in range(2)]
        htmp = [at(f"htmp{s}", ZT + 5024 * s, [128, NP]) for s in range(2)]
        cnt = [at(f"cnt{s}", ZT + 5024 * s, [T, N]) for s in range(2)]
        hout = at("hout", ZT + 10048, [T, NT * 128])
        diag = at("diag", ZT + 10048, [T, NT, T])
        dinv_b = at("dinv_b", ZT + 10048 + 5120, [128, NP])
        q_p = [at(f"qT_{'hl'[q]}", R + 5024 * q, [128, NP], F32R) for q in range(2)]
        k_p = [at(f"kT_{'hl'[q]}", R + 10048 + 5024 * q, [128, NP], F32R) for q in range(2)]
        vt = at("vT", R + 20096, [128, NP])
        v_p = [at(f"v_{'hl'[q]}", R + 25120 + 10240 * q, [T, NT, 256], F32R) for q in range(2)]
        qp_p = [at(f"qp_{'hl'[q]}", R + 45600 + 10048 * q, [128, 2, NP], F32R) for q in range(2)]
        xn_in = [at(f"xn_in{s}", R + 45600 + 4096 * s, [T, D]) for s in range(2)]
        kk_p = [[at(f"kk_{'hl'[q]}{s}", R + 65696 + 4096 * s + 2048 * q, [T, 2 * FEAT], F32R)
                 for q in range(2)] for s in range(3)]
        s_p = [at(f"s_{'hl'[q]}", R + 73888 + 2048 * q, [128, 2, 2, 128], F32R) for q in range(2)]
        num = at("num", R + 77984, [128, NP])
        nrm = at("nrm", R + 83008, [128, NP])
        att_p = [at(f"att_{'hl'[q]}", R + 83008 + 5024 * q, [128, NP], F32R) for q in range(2)]
        proj_raw = at("proj_raw", R + 93056, [128, 2 * FEAT])
        proj_p = [at(f"proj_{'hl'[q]}", R + 95104 + 2048 * q, [128, 2 * FEAT], F32R) for q in range(2)]
        kvt = at("kvt", R + 99200, [128, 2 * FEAT])
        acc = at("acc", R, [T, NT, D])
        gnn_in = [at(f"gnn_in{s}", R + 40960 + 5024 * s, [128, NP]) for s in range(2)]
        otmp = [at(f"otmp{s}", R + 51008 + 5024 * s, [128, NP]) for s in range(2)]
        x_in = [at(f"x_in{s}", R + 61056 + 5120 * s, [T, NT, 128]) for s in range(2)]
        flat = [at(f"flat{s}", R + 40960 + 4096 * s, [T, D]) for s in range(2)]
        l2st = at("l2st", R + 82944, [T, NT, KD * 6])
        lg = at("lg", R + 61056, [T, NT, EXP])
        lgt = at("lgt", R + 71680, [2 * EXP, NP])
        lg2 = at("lg2", R + 76800, [T, NT * 2 * EXP])
        cmp_gt = at("cmp_gt", R + 61376, [T, NT, EXP * EXP])
        cmp_ge = at("cmp_ge", R + 66080, [T, NT, EXP * EXP])
        tie_t = at("tie_t", R + 95680, [T, EXP * EXP])
        rank = at("rank", R + 95936, [T, NT, EXP])
        rsm = at("rsm", R + 96256, [T, 8 * NT])
        rtmp = at("rtmp", R + 96576, [T, NT, EXP])

        xe_p = [[at(f"xe_{'hl'[q]}{s}", 26880 * s + 13440 * q, [128, KD, CAP], F32R) for q in range(2)]
                for s in range(2)]
        ws_p = [[at(f"ws_{'hl'[q]}{s}", 53760 + 8192 * s + 4096 * q, [128, KD, 128], F32R)
                 for q in range(2)] for s in range(3)]
        pos = at("pos", 78336, [T, NT * EXP])
        rec = at("rec", 78656, [T, NT, EXP, 6], BF16)
        ws_raw = [at(f"ws_raw{s}", BIG + 4096 * s, [128, KD * 128]) for s in range(4)]
        w2_raw = at("w2_raw", BIG + 16384, [128, 2, D])
        xg = [at(f"xg{s}", R + 16384 * s, [RT_, NRT, D]) for s in range(2)]
        y = [at(f"y{i}", R + 32768 + 4096 * i, [RT_, D]) for i in range(NRT)]
        w2_p = [[at(f"w2_{'hl'[q]}{s}", R + 49152 + 16384 * s + 8192 * q, [128, 2, D], F32R)
                 for q in range(2)] for s in range(2)]
        a_p = [at(f"a_{'hl'[q]}", R + 81920 + 3360 * q, [128, 2, CAP], F32R) for q in range(2)]
        sil = at("sil", R + 88640, [128, CAP])
        actt = at("actt", R + 90336, [128, CAP])
        hit = at("hit", R + 92032, [T, NT, CAP], BF16)
        place_iota = at("place_iota", R + 100448, [T, CAP], F16)
        before_t = at("before_t", R + 101312, [T, 2 * T], F16)
        sel = at("sel", R + 101824, [T, NT * EXP], F16)
        tok_t = at("tok_t", R + 97280, [T, NT, 3])

        slot = [ctx.enter_context(nc.psum_tensor(f"slot{s}", [128, 1536], F32)) for s in range(2)]
        kvb = ctx.enter_context(nc.psum_tensor("kvb", [128, 512], F32))
        lsb = ctx.enter_context(nc.psum_tensor("lsb", [128, 512], F32))
        wide = [ps_[:, 0:1024] for ps_ in slot]
        narrow = [slot[0][:, 1024:1024 + CAP], slot[1][:, 1024:1024 + CAP], kvb[:, :CAP]]

        xn_d = nc.dram_tensor("xn_d", [N, D], F32, kind="Internal").ap()
        xs_d = [nc.dram_tensor(f"xs_d{i}", [KD, T, NT * 128], F32, kind="Internal").ap() for i in range(2)]
        gnn_d = nc.dram_tensor("gnn_d", [KD, 128, NP], F32, kind="Internal").ap()
        at_d = nc.dram_tensor("at_d", [KD, 2, 128, NP], F32, kind="Internal").ap()

        flat_d = nc.dram_tensor("flat_d", [N + CAP, D], F32, kind="Internal").ap()

        const_in = sem("const_in")
        edges_in = sem("edges_in")
        memset_done = sem("memset_done")
        chain = sem("chain")
        round_chain = sem("round_chain")
        sel_ready = sem("sel_ready")
        bounds_ready = sem("bounds_ready")
        keys_ready = sem("keys_ready")
        keys_max = sem("keys_max")
        oh_ready = [sem(f"oh_ready{j}") for j in range(GC)]
        oh_used = [sem(f"oh_used{j}") for j in range(GC)]
        diag_added = sem("diag_added")
        x_landed = [sem(f"x_landed{s}") for s in range(2)]
        x_used = sem("x_used")
        achain = sem("achain")
        ln_sums = sem("ln_sums")
        rstd_ready = sem("rstd_ready")
        xn_stored = [sem(f"xn_stored{s}") for s in range(2)]
        pe_landed = [sem(f"pe_landed{s}") for s in range(2)]
        x0_ready = sem("x0_ready")
        x0_stored = [sem(f"x0_stored{s}") for s in range(2)]
        deg_sqrt = sem("deg_sqrt")
        diag_ready = sem("diag_ready")
        dinv_ready = sem("dinv_ready")
        slab_landed = [sem(f"slab_landed{s}") for s in range(2)]
        xs_landed = [sem(f"xs_landed{s}") for s in range(2)]
        xs_scaled = sem("xs_scaled")
        z_scaled = sem("z_scaled")
        h_biased = sem("h_biased")
        bn_ready = sem("bn_ready")
        std_ready = sem("std_ready")
        bn_affine = sem("bn_affine")
        h_stored = sem("h_stored")
        gnn_stored = [sem(f"gnn_stored{s}") for s in range(2)]
        xn_landed = [sem(f"xn_landed{s}") for s in range(2)]
        kv_full = sem("kv_full")
        s_full = sem("s_full")
        att_stored = sem("att_stored")
        at_landed = sem("at_landed")
        gnn_landed = [sem(f"gnn_landed{s}") for s in range(2)]
        xr_landed = [sem(f"xr_landed{s}") for s in range(2)]
        ln2_var = sem("ln2_var")
        ln2_std = sem("ln2_std")
        exp_in = sem("exp_in")
        exp_out = sem("exp_out")
        blanks_in = sem("blanks_in")
        lists_in = sem("lists_in")
        flat_stored = [sem(f"flat_stored{s}") for s in range(2)]
        x2_stored = sem("x2_stored")
        rounds_ready = sem("rounds_ready")
        ws_landed = [sem(f"ws_landed{s}") for s in range(4)]
        w2_landed = sem("w2_landed")
        hits_ready = sem("hits_ready")
        gathered = [[sem(f"gathered{s}_{i}") for i in range(NRT)] for s in range(2)]
        act_made = sem("act_made")
        sp_passed = sem("sp_passed")
        pool_passed = sem("pool_passed")
        added = sem("added")
        expert_full = sem("expert_full")
        expert_act = sem("expert_act")
        expert_dve = sem("expert_dve")
        psum_full = sem("psum_full")
        slot_free = [sem(f"slot_free{s}") for s in range(2)]
        act_done = sem("act_done")
        dve_done = sem("dve_done")
        wr_zeroed = sem("wr_zeroed")
        wr_hi = sem("wr_hi")
        wr_lo = sem("wr_lo")
        proj_zeroed = sem("proj_zeroed")
        proj_landed = sem("proj_landed")

        def chunks(ap):
            return ap.rearrange("p (q c) -> p q c", c=CW)

        def cols(ps, rows_=128):
            return ps[:rows_, :].rearrange("p (q c) -> p q c", c=512)[:, :, :CW]

        def blocks(ps, n, w, rows_):
            return ps[:rows_, :n * 128].rearrange("p (j c) -> p j c", c=128)[:, :, :w]

        def v_cols(v):
            return v.rearrange("p j (h c) -> p j h c", c=64)[:, :, 0:4:3, :]

        def v_psum(ps):
            return ps[:T, :NT * 128].rearrange("p (j h c) -> p j h c", h=2, c=64)

        block = ctx.enter_context(nc.Block())

        @block.sync
        def _(sp):
            sp.dma_start(dsti[:, :], dst_cols).then_inc(edges_in, 16)
            sp.dma_start(srci[:, :], src_cols).then_inc(edges_in, 16)
            sp.dma_start(grp_i[:, :], dst_groups).then_inc(edges_in, 16)
            sp.dma_start(iota_t[:, :], iota).then_inc(edges_in, 16)
            sp.dma_start(gno[:, :], group_no[:, 0:2]).then_inc(edges_in, 16)
            sp.dma_start(tile_no[:, :], group_no[:, 2:2 + 2 * NT]).then_inc(edges_in, 16)
            sp.dma_start(ident[:, :], consts).then_inc(const_in, 16)
            sp.dma_start(rows[:, :], feat_rows).then_inc(const_in, 16)
            sp.dma_start(wr_raw[:, :], wr).then_inc(const_in, 16)
            for n in range(2):
                sp.dma_start(slab_raw[n][:, :], slabs[n]).then_inc(slab_landed[n], 16)

            def load_xs(layer, t):
                s = t % 2
                if layer == 1 and t == 0:
                    for r in range(2):
                        sp.wait_ge(x0_stored[r], 16 * NT // 2)
                if layer == 2:
                    sp.wait_ge(h_stored, 16 * (t + 1))
                sp.dma_start(xs_raw[s][:, :, :].rearrange("p j c -> p (j c)"),
                             xs_d[layer - 1][t]).then_inc(xs_landed[s], 16)

            for k in ORDER:
                if k[0] == "LNA":
                    for i in range(NT):
                        if i >= 2:
                            sp.wait_ge(x_used, i - 1)
                        sp.dma_start(xt[i % 2][:, :], x[T * i:T * i + T, :]).then_inc(x_landed[i % 2], 16)
                elif k[0] == "LNB":
                    i = k[1]
                    sp.wait_ge(act_done, ACTED[k])
                    sp.dma_start(xn_d[T * i:T * i + T, :], xn[i % 2][:, :]).then_inc(xn_stored[i % 2], 16)
                    if i >= 2:
                        sp.wait_ge(x0_ready, i - 1)
                    sp.dma_start(pet[i % 2][:, :], pe[T * i:T * i + T, :]).then_inc(pe_landed[i % 2], 16)
                    sp.wait_ge(x0_ready, i + 1)
                    sp.dma_start(xs_d[0].rearrange("f p (j c) -> j p f c", c=128)[i],
                                 x0t[i % 2][:, :].rearrange("p (f c) -> p f c", c=128)
                                 ).then_inc(x0_stored[i % 2], 16)
                elif k[0] == "DEG":
                    load_xs(1, 0)
                    load_xs(1, 1)
                    sp.dma_start(flat_d[N:N + CAP, :], blank).then_inc(blanks_in, 16)
                    sp.dma_start(out[N:N + CAP, :], blank).then_inc(blanks_in, 16)
                elif k[0] == "ZP":
                    _, layer, t = k
                    if layer == 2 and t == 0:
                        load_xs(2, 0)
                        load_xs(2, 1)
                    if t + 2 < KD:
                        sp.wait_ge(dve_done, DVED[k])
                        load_xs(layer, t + 2)
                elif k[0] == "P":
                    n = k[1]
                    if n + 2 < len(SLABS):
                        sp.wait_ge(dve_done, DVED[k])
                        sp.dma_start(slab_raw[n % 2][:, :], slabs[n + 2]).then_inc(slab_landed[n % 2], 16)
                elif k[0] == "HT":
                    sp.wait_ge(act_done, ACTED[k])
                    sp.dma_start(xs_d[1][k[1]], hout[:, :]).then_inc(h_stored, 16)
                elif k[0] == "H" and k[1] == 2:
                    f = k[2]
                    sp.wait_ge(act_done, ACTED[k])
                    sp.dma_start(gnn_d[f], htmp[f % 2][:, :]).then_inc(gnn_stored[f % 2], 16)
                    if f == 2:
                        for i in range(2):
                            sp.wait_ge(xn_stored[i], 16 * NT // 2)
                            sp.dma_start(xn_in[i][:, :], xn_d[T * i:T * i + T, :]).then_inc(xn_landed[i], 16)
                elif k[0] == "XT":
                    i = k[1]
                    if i + 2 < NT:
                        sp.wait_ge(psum_full, FULL[k])
                        sp.dma_start(xn_in[i % 2][:, :], xn_d[T * (i + 2):T * (i + 3), :]
                                     ).then_inc(xn_landed[i % 2], 16)
                elif k[0] == "MP":
                    sp.wait_ge(proj_zeroed, 1)
                    for h in range(2):
                        sp.dma_start(proj_raw[DH * h:DH * h + DH, FEAT * h:FEAT * h + FEAT], proj
                                     ).then_inc(proj_landed, 16)
                elif k[0] == "RH":
                    p = k[1]
                    sp.wait_ge(dve_done, DVED[k])
                    if p < PAIRS - 1:
                        for q in range(2):
                            sp.dma_start(at_d[p, q], att_p[q][:, :].bitcast(F32)).then_inc(att_stored, 16)
                    if p == PAIRS - 2:
                        sp.wait_ge(psum_full, FULL[("V", PAIRS - 1)])
                        sp.wait_ge(att_stored, 32 * (PAIRS - 1))
                        for t in range(PAIRS - 1):
                            for q in range(2):
                                sp.dma_start(big[q][:, t, :].bitcast(F32), at_d[t, q]).then_inc(at_landed, 16)
                    if p == PAIRS - 1:
                        for s in range(2):
                            sp.dma_start(gnn_in[s][:, :], gnn_d[s]).then_inc(gnn_landed[s], 16)
                            sp.dma_start(x_in[s][:, :, :],
                                         x.rearrange("(j p) (f c) -> f p j c", p=T, c=128)[s]
                                         ).then_inc(xr_landed[s], 16)
                elif k[0] == "O":
                    f = k[1]
                    if f + 2 < KD:
                        sp.wait_ge(dve_done, DVED[k])
                        sp.dma_start(gnn_in[f % 2][:, :], gnn_d[f + 2]).then_inc(gnn_landed[f % 2], 16)
                elif k[0] == "OT":
                    f = k[1]
                    if f + 2 < KD:
                        sp.wait_ge(dve_done, DVED[k])
                        sp.dma_start(x_in[f % 2][:, :, :],
                                     x.rearrange("(j p) (f c) -> f p j c", p=T, c=128)[f + 2]
                                     ).then_inc(xr_landed[f % 2], 16)
                    if f == KD - 1:
                        sp.wait_ge(dve_done, DVED[k])
                        sp.dma_start(tie_t[:, :], tie).then_inc(const_in, 16)
                        sp.dma_start(place_iota[:, :], iota[:, 0:CAP]).then_inc(lists_in, 16)
                        sp.dma_start(before_t[:, :], before).then_inc(lists_in, 16)
                        sp.dma_start(place_no[:, :], places).then_inc(lists_in, 16)
                        sp.dma_start(tok_t[:, :, :].rearrange("p j c -> p (j c)"), tokens).then_inc(lists_in, 16)
                elif k[0] == "FL":
                    j = k[1]
                    sp.wait_ge(dve_done, DVED[k])
                    sp.dma_start(flat_d[T * j:T * j + T, :], flat[j % 2][:, :]).then_inc(flat_stored[j % 2], 16)
            for j in range(NT):
                sp.dma_start(out[T * j:T * j + T, :], acc[:, j, :]).then_inc(x2_stored, 16)
            sp.wait_ge(rounds_ready, 1)
            rounds = sp.value_load(rounds_n[0:1, 0:1], min_val=1, max_val=ROUNDS)
            with sp.Fori(0, rounds) as r:

                def load_ws(m):
                    sp.dma_start(ws_raw[m % 4][:, :], w1[m]).then_inc(ws_landed[m % 4], 16)

                def load_w2(e):
                    sp.dma_start(w2_raw[:, :, :].rearrange("p a c -> p (a c)"), w2[e]).then_inc(w2_landed, 16)

                for m in range(4):
                    load_ws(m)
                load_w2(0)
                for k in ROUND:
                    if k[0] == "WP" and k[1] + 4 < NWS:
                        sp.wait_ge(expert_dve, r * len(R_DVE) + R_DVE[k])
                        load_ws(k[1] + 4)
                    elif k[0] == "W2P" and k[1] + 1 < EXP:
                        sp.wait_ge(expert_dve, r * len(R_DVE) + R_DVE[k])
                        load_w2(k[1] + 1)
                sp.wait_ge(expert_dve, (r + 1) * len(R_DVE))
                sp.sem_inc(sp_passed, 1)

        @block.gpsimd
        def _(pool):
            pool.memset(zeros[:, :], 0.0).then_inc(memset_done, 1)
            pool.memset(onesf[:, :], 1.0).then_inc(memset_done, 1)
            pool.memset(eps[:, :], LN_EPS).then_inc(memset_done, 1)
            pool.memset(adj[:, :, N:NP].bitcast(F32), 0.0).then_inc(memset_done, 1)
            pool.memset(dinv_b[:, N:NP], 0.0).then_inc(memset_done, 1)
            pool.memset(wr_p[0][:, :].bitcast(F32), 0.0)
            pool.memset(wr_p[1][:, :].bitcast(F32), 0.0).then_inc(wr_zeroed, 1)
            pool.wait_ge(keys_ready, 1)
            pool.partition_all_reduce(key_m[:, :], key_b[:, :], NG, bass.bass_isa.ReduceOp.max
                                      ).then_inc(keys_max, 1)
            for k in ORDER:
                if k[0] == "G":
                    b = k[1]
                    if b == 0:
                        pool.wait_ge(const_in, 16 * 3)
                    pool.wait_ge(act_done, ACTED[k])
                    blk = cnt[b % 2][:, T * b:T * b + T]
                    pool.tensor_tensor(blk, blk, ident[:T, :T], ALU.add).then_inc(diag_added, 1)
                elif k[0] == "MP":
                    pool.wait_ge(dve_done, DVED[("XT", 0)])
                    for s in range(2):
                        pool.wait_ge(gnn_stored[s], 16 * KD // 2)
                    for q in range(2):
                        pool.memset(v_p[q][:, :, 64:192].bitcast(F32), 1.0 - q)
                    pool.memset(proj_raw[:, :], 0.0).then_inc(proj_zeroed, 1)
                elif k[0] == "LNB":
                    i = k[1]
                    pool.wait_ge(act_done, ACTED[k])
                    pool.wait_ge(pe_landed[i % 2], 16 * (i // 2 + 1))
                    if i >= 2:
                        pool.wait_ge(x0_stored[i % 2], 16 * (i // 2))
                    pool.tensor_tensor(x0t[i % 2][:, :], xn[i % 2][:, :], pet[i % 2][:, :], ALU.add
                                       ).then_inc(x0_ready, 1)

            pool.wait_ge(blanks_in, 32)
            pool.wait_ge(x2_stored, 16 * NT)
            for s in range(2):
                pool.wait_ge(flat_stored[s], 16 * NT // 2)
            pool.wait_ge(rounds_ready, 1)
            rounds = pool.value_load(rounds_n[0:1, 0:1], min_val=1, max_val=ROUNDS)
            with pool.Fori(0, rounds) as r:

                def gather(e):
                    pool.wait_ge(expert_dve, r * len(R_DVE) + R_DVE[("LS", e)])
                    if e >= 2:
                        pool.wait_ge(expert_full, r * len(R_FULL) + R_FULL[("XE", e - 2, NRT - 1)])
                    pool.sem_inc(pool_passed, 1)
                    for i in range(NRT):
                        pool.indirect_dma_start(xg[e % 2][:, i, :], None, flat_d,
                                                bass.IndirectOffsetOnAxis(ap=token[e % 4][:, i:i + 1], axis=0)
                                                ).then_inc(gathered[e % 2][i], 16)

                gather(0)
                gather(1)
                for e in range(EXP):
                    if e + 2 < EXP:
                        gather(e + 2)
                    if e:
                        pool.wait_ge(added, r * (16 * NRT * EXP) + 16 * NRT * e)
                    for i in range(NRT):
                        pool.wait_ge(expert_act, r * len(R_ACT) + R_ACT[("OUT", e, i)])
                        pool.sem_inc(pool_passed, 1)
                        pool.indirect_dma_start(out, bass.IndirectOffsetOnAxis(ap=token[e % 4][:, i:i + 1], axis=0),
                                                y[i][:, :], None, compute_op=ALU.add).then_inc(added, 16)
                pool.wait_ge(added, (r + 1) * (16 * NRT * EXP))

        @block.scalar
        def _(act):
            links = [0]

            def link(ins):
                links[0] += 1
                ins.then_inc(achain, 1)
                act.wait_ge(achain, links[0])

            def done(k, ins, free=True):
                ins.then_inc(act_done, 1)

            copy = lambda o, i, **kw: act.activation(o, i, ACT.Copy, **kw)

            for k in ORDER:
                kind = k[0]
                if kind not in ACT_KINDS and kind not in ("LNA", "LNS", "DEG", "LN2"):
                    continue
                if kind in PSUM_KINDS:
                    u, s = FULL[k], slot_of(k)
                    ps = slot[s]
                    if kind not in ("Z", "VA"):
                        act.wait_ge(psum_full, u)
                if kind == "LNA":
                    for i in range(NT):
                        act.wait_ge(x_landed[i % 2], 16 * (i // 2 + 1))
                        link(act.activation(dx[:, i, :], xt[i % 2][:, :], ACT.Copy, accum_out=xsum[:, i:i + 1]))
                        link(copy(nmean[:, i:i + 1], xsum[:, i:i + 1], scale=-1.0 / D))
                        link(act.activation(dx[:, i, :], xt[i % 2][:, :], ACT.Identity, bias=nmean[:, i:i + 1]))
                        ins = act.activation(xt[i % 2][:, :], dx[:, i, :], ACT.Square, accum_out=vsum[:, i:i + 1])
                        ins.then_inc(x_used, 1)
                    act.wait_ge(x_used, NT)
                    act.wait_ge(memset_done, 5)
                    act.activation(std[:T, :], vsum[:, :], ACT.Sqrt, bias=eps[:T, :], scale=1.0 / D
                                   ).then_inc(ln_sums, 1)
                elif kind == "LNB":
                    i = k[1]
                    if i == 0:
                        act.wait_ge(rstd_ready, 1)
                    if i >= 2:
                        act.wait_ge(xn_stored[i % 2], 16 * (i // 2))
                        act.wait_ge(x0_ready, i - 1)
                    copy(xn[i % 2][:, :], dx[:, i, :], scale=rstd[:, i:i + 1]).then_inc(act_done, 1)
                elif kind == "G":
                    b = k[1]
                    copy(cnt[b % 2][:, 0:2 * CW].rearrange("p (q c) -> p q c", c=CW),
                         ps[:T, :1024].rearrange("p (q c) -> p q c", c=512)[:, :, :CW],
                         accum_out=degs[:, 2 * b:2 * b + 1])
                    ins = copy(cnt[b % 2][:, 2 * CW:N], ps[:T, 1024:1024 + N - 2 * CW],
                               accum_out=degs[:, 2 * b + 1:2 * b + 2])
                    ins.then_inc(act_done, 1)
                elif kind == "GT":
                    b = k[1]
                    copy(adj[:, :, T * b:T * b + T], blocks(ps, NT, T, T)).then_inc(act_done, 1)
                elif kind == "DEG":
                    act.wait_ge(dinv_ready, 1)
                    act.activation(std[:T, :], nw[:T, 0:NT], ACT.Sqrt).then_inc(deg_sqrt, 1)
                    act.wait_ge(const_in, 16 * 3)
                    act.wait_ge(wr_zeroed, 1)
                    for q in range(2):
                        copy(wr_p[q][:, 0:KD * 2 * EXP].rearrange("p (k e) -> p k e", e=2 * EXP)[:, :, 0:EXP],
                             wr_raw[:, :].rearrange("p (k e) -> p k e", e=EXP)).then_inc(wr_hi, 1)
                elif kind == "DB":
                    copy(dinv_b[:, 0:N].rearrange("p (j c) -> p j c", c=T), blocks(ps, NT, T, 128)
                         ).then_inc(act_done, 1)
                elif kind == "ZP":
                    _, layer, t = k
                    act.wait_ge(xs_scaled, (layer - 1) * KD + t + 1)
                    if t >= 2:
                        act.wait_ge(psum_full, FULL[("Z", layer, t - 2)])
                    copy(xs_p[t % 2][0][:, :, :], xs_raw[t % 2][:, :, :]).then_inc(act_done, 1)
                elif kind == "Z":
                    _, layer, t = k
                    act.wait_ge(z_scaled, (layer - 1) * KD + t + 1)
                    copy(big[0][:, t, :], ztmp[t % 2][:, :]).then_inc(act_done, 1)
                elif kind == "P":
                    n = k[1]
                    if n == 0:
                        act.wait_ge(wr_lo, 1)
                    act.wait_ge(slab_landed[n % 2], 16 * (n // 2 + 1))
                    if n >= 2:
                        act.wait_ge(psum_full, FULL[SLABS[n - 2]])
                    copy(slab_p[n % 2][0][:, :, :], slab_raw[n % 2][:, :].rearrange("p (k c) -> p k c", c=128)
                         ).then_inc(act_done, 1)
                elif kind == "H" and k[1] == 1:
                    f = k[2]
                    h = htmp[f % 2]
                    act.activation(chunks(h[:, :]), cols(ps), ACT.Identity, bias=b1c[:, f:f + 1]
                                   ).then_inc(h_biased, 1)
                    act.wait_ge(bn_ready, f + 1)
                    act.activation(std[:, 0:1], bmv[:, 1:2], ACT.Sqrt, bias=eps[:, :]).then_inc(std_ready, 1)
                    act.wait_ge(bn_affine, f + 1)
                    act.activation(h[:, :], h[:, :], ACT.Relu, bias=bsc[:, 1:2], scale=bsc[:, 0:1]
                                   ).then_inc(act_done, 1)
                elif kind == "H":
                    f = k[2]
                    if f >= 2:
                        act.wait_ge(gnn_stored[f % 2], 16 * (f // 2))
                    act.activation(chunks(htmp[f % 2][:, :]), cols(ps), ACT.Relu, bias=b2c[:, f:f + 1]
                                   ).then_inc(act_done, 1)
                elif kind == "HT":
                    if k[1]:
                        act.wait_ge(h_stored, 16 * k[1])
                    copy(hout[:, :], ps[:T, :NT * 128]).then_inc(act_done, 1)
                elif kind in ("XT", "FT"):
                    i = k[1]
                    copy(big[0][:, :, T * i:T * i + T], blocks(ps, KD, T, 128)).then_inc(act_done, 1)
                elif kind == "V":
                    copy(chunks(vt[:, :]), cols(ps)).then_inc(act_done, 1)
                elif kind == "VT":
                    copy(v_cols(v_p[0][:, :, :]), v_psum(ps)).then_inc(act_done, 1)
                elif kind in ("K", "Q"):
                    copy(chunks((k_p if kind == "K" else q_p)[0][:, :]), cols(ps)).then_inc(act_done, 1)
                elif kind == "KK":
                    act.activation(kk_p[k[2] % 3][0][:, :], ps[:T, :2 * FEAT], ACT.Relu).then_inc(act_done, 1)
                elif kind == "KC":
                    act.wait_ge(kv_full, k[1] + 1)
                    copy(kvt[:, :], kvb[:, :]).then_inc(act_done, 1)
                elif kind == "S":
                    act.wait_ge(s_full, k[1] + 1)
                    copy(s_p[0][:, :, :, :].rearrange("p h f c -> p (h f c)"), lsb[:, :]).then_inc(act_done, 1)
                elif kind == "MP":
                    act.wait_ge(proj_landed, 32)
                    copy(proj_p[0][:, :], proj_raw[:, :]).then_inc(act_done, 1)
                elif kind == "QP":
                    act.activation(chunks(qp_p[0][:, k[3], :]), cols(ps), ACT.Relu).then_inc(act_done, 1)
                elif kind == "AT":
                    p, h = k[1], k[2]
                    if p == 0 and h == 0:
                        for s_ in range(2):
                            act.wait_ge(gnn_stored[s_], 16 * KD // 2)
                    if p and h == 0:
                        act.wait_ge(dve_done, DVED[("RH", p - 1)])
                        act.wait_ge(att_stored, 32 * p)
                    o, a, b = 64 * h, 64 * h, 64 - 64 * h
                    copy(chunks(num[o:o + 64, :]), cols(ps)[a:a + 64])
                    ins = copy(chunks(nrm[o:o + 64, :]), cols(ps)[b:b + 64], bias=ATT_EPS)
                    ins.then_inc(act_done, 1)
                elif kind == "RH":
                    p = k[1]
                    act.wait_ge(dve_done, DVED[("RC", p)])
                    hi = att_p[0][:, :] if p < PAIRS - 1 else big[0][:, p, :]
                    copy(hi, num[:, :]).then_inc(act_done, 1)
                elif kind == "LN2":
                    act.wait_ge(ln2_var, 1)
                    act.activation(std[:T, :], l2mv[:, 1:2 * NT:2], ACT.Sqrt, bias=eps[:T, :]).then_inc(ln2_std, 1)
                elif kind == "R":
                    copy(chunks(lgt[:, :]), cols(ps, 2 * EXP)).then_inc(act_done, 1)
                elif kind == "RT":
                    copy(lg2[:, :], ps[:T, :NT * 2 * EXP]).then_inc(act_done, 1)
                    act.wait_ge(exp_in, 1)
                    act.activation(rsm[:, 3 * NT:4 * NT], rsm[:, 2 * NT:3 * NT], ACT.Exp).then_inc(exp_out, 1)

            act.wait_ge(rounds_ready, 1)
            rounds = act.value_load(rounds_n[0:1, 0:1], min_val=1, max_val=ROUNDS)
            with act.Fori(0, rounds) as r:

                def full(k):
                    act.wait_ge(expert_full, r * len(R_FULL) + R_FULL[k])

                for k in ROUND:
                    kind = k[0]
                    if kind == "WP":
                        m = k[1]
                        act.wait_ge(ws_landed[m % 4], r * (16 * NWS // 4) + 16 * (m // 4 + 1))
                        if m >= 3:
                            full(NARROW_KEYS[m - 3])
                        copy(ws_p[m % 3][0][:, :, :], ws_raw[m % 4][:, :].rearrange("p (k c) -> p k c", c=128)
                             ).then_inc(expert_act, 1)
                    elif kind == "W2P":
                        e = k[1]
                        act.wait_ge(w2_landed, r * (16 * EXP) + 16 * (e + 1))
                        if e >= 2:
                            full(("OUT", e - 2, NRT - 1))
                        copy(w2_p[e % 2][0][:, :, :], w2_raw[:, :, :]).then_inc(expert_act, 1)
                    elif kind == "XE":
                        e, i = k[1:]
                        full(k)
                        copy(xe_p[e % 2][0][:, :, RT_ * i:RT_ * i + RT_],
                             blocks(wide[(WIDE[k] - 1) % 2], KD, RT_, 128)).then_inc(expert_act, 1)
                    elif kind == "GA":
                        n = 2 * k[1] + k[2]
                        full(k)
                        if n:
                            act.wait_ge(act_made, r * (2 * EXP) + n)
                        act.activation(sil[:, :], narrow[(NARROW[k] - 1) % 3], ACT.Silu
                                       ).then_inc(expert_act, 1)
                    elif kind == "VA":
                        e, t = k[1:]
                        n = 2 * e + t
                        act.wait_ge(act_made, r * (2 * EXP) + n + 1)
                        if e and t == 0:
                            full(("OUT", e - 1, NRT - 1))
                        copy(a_p[0][:, t, :], actt[:, :]).then_inc(expert_act, 1)
                    elif kind == "OUT":
                        e, i = k[1:]
                        full(k)
                        if e:
                            act.wait_ge(added, r * (16 * NRT * EXP) + 16 * NRT * e)
                        copy(y[i][:, :], wide[(WIDE[k] - 1) % 2][:RT_, :], scale=share[e % 4][:, i:i + 1]
                             ).then_inc(expert_act, 1)
                act.wait_ge(added, (r + 1) * (16 * NRT * EXP))

        @block.vector
        def _(dve):
            links = [0]

            def link(ins):
                links[0] += 1
                ins.then_inc(chain, 1)
                dve.wait_ge(chain, links[0])

            def tt(o, a, b, op):
                return dve.tensor_tensor(o, a, b, op)

            def ts(o, a, s1, op0, s2=None, op1=None):
                return dve.tensor_scalar(o, a, s1, s2, op0, op1) if op1 is not None else \
                    dve.tensor_scalar(o, a, s1, None, op0)

            def newton(res, v, root, n, rows_, tmp):
                a, b = tmp[:rows_, 0:n], tmp[:rows_, n:2 * n]
                link(dve.reciprocal(a, root))
                link(tt(b, a, a, ALU.mult))
                link(tt(b, b, v, ALU.mult))
                link(ts(b, b, -0.5, ALU.mult, 1.5, ALU.add))
                return tt(res, a, b, ALU.mult)

            def find_bounds():
                dve.wait_ge(edges_in, 16 * 6)
                dve.tensor_copy(dstf[:, :], dsti[:, :])
                dve.tensor_copy(srcf[:, :], srci[:, :])
                link(dve.tensor_copy(grp_f[:, :], grp_i[:, :]))
                dve.tensor_reduce(gmm[:, 0:1], grp_f[:, :], AX.X, ALU.min)
                link(dve.tensor_reduce(gmm[:, 1:2], grp_f[:, :], AX.X, ALU.max))
                link(ts(key_a[:, :], tile_no[:, 0:NT], gmm[:, 1:2], ALU.is_le))
                link(dve.scalar_tensor_tensor(out=key_a[:, :], in0=tile_no[:, NT:2 * NT], scalar=gmm[:, 0:1],
                                              in1=key_a[:, :], op0=ALU.is_gt, op1=ALU.mult))
                ts(key_b[:, 0:NT], key_a[:, :], gno[:, 1:2], ALU.mult)
                ts(key_b[:, NT:2 * NT], key_a[:, :], gno[:, 0:1], ALU.mult).then_inc(keys_ready, 1)
                dve.wait_ge(keys_max, 1)
                lo, hi, n_, st, w = (lims[0:1, NT * i:NT * i + NT] for i in range(5))
                link(ts(lo, key_m[0:1, 0:NT], -1.0, ALU.mult, float(NG), ALU.add))
                link(ts(lo, lo, float(NG - 1), ALU.min))
                link(ts(hi, lo, 1.0, ALU.add))
                link(tt(hi, hi, key_m[0:1, NT:2 * NT], ALU.max))
                link(tt(n_, hi, lo, ALU.subtract))
                cur, nxt = n_, st
                step = 1
                while step < NT:
                    dve.tensor_copy(nxt[:, 0:step], cur[:, 0:step])
                    link(tt(nxt[:, step:], cur[:, step:], cur[:, :NT - step], ALU.add))
                    cur, nxt = nxt, (w if nxt is st else st)
                    step *= 2
                link(tt(n_, hi, cur, ALU.subtract))
                dve.tensor_copy(bounds[:, 0:NT], cur)
                dve.tensor_copy(bounds[:, NT:2 * NT], n_).then_inc(bounds_ready, 1)

            find_bounds()
            dve.wait_ge(bounds_ready, 1)
            start = 0
            for k in ORDER:
                kind = k[0]
                if kind not in DVE_KINDS and kind not in ("G", "LNS", "DEG", "H", "LN2"):
                    continue
                if kind in PSUM_KINDS:
                    u, s = FULL[k], slot_of(k)
                    ps = slot[s]
                if kind == "G":
                    b = k[1]
                    end = dve.value_load(bounds[0:1, b:b + 1], min_val=1, max_val=NG * NT)
                    shift = dve.value_load(bounds[0:1, NT + b:NT + b + 1], min_val=-NG * NT, max_val=NG)
                    with dve.Fori(start, end) as r:
                        group = nc.s_assert_within(r + shift, 0, NG - 1, skip_runtime_bounds_check_because=
                                                   "find_bounds keeps every group within the edge list")
                        for j in range(GC):
                            c = group * GC + j
                            dve.wait_ge(oh_used[j], r + 1)
                            ts(oh_src[j][:, :], iota_t[:, :], srcf[:, bass.ds(c, 1)], ALU.is_equal)
                            ts(oh_dst[j][:, :], iota_t[:, T * b:T * b + T], dstf[:, bass.ds(c, 1)], ALU.is_equal
                               ).then_inc(oh_ready[j], 1)
                    start = end
                elif kind == "LNS":
                    dve.wait_ge(ln_sums, 1)
                    link(ts(nw[:T, 2 * NT:3 * NT], vsum[:, :], 1.0 / D, ALU.mult, LN_EPS, ALU.add))
                    newton(rstd[:, :], nw[:T, 2 * NT:3 * NT], std[:T, :], NT, T, nw[:, 3 * NT:]
                           ).then_inc(rstd_ready, 1)
                elif kind == "DEG":
                    dve.wait_ge(act_done, ACTED[("G", NT - 1)])
                    link(tt(nw[:T, 0:NT], degs[:, 0:2 * NT:2], degs[:, 1:2 * NT:2], ALU.add))
                    ts(nw[:T, 0:NT], nw[:T, 0:NT], 1.0, ALU.add).then_inc(dinv_ready, 1)
                    dve.wait_ge(deg_sqrt, 1)
                    link(newton(dinv[:, :], nw[:T, 0:NT], std[:T, :], NT, T, nw[:, NT:3 * NT]))
                    tt(diag[:, :, :], ident[:T, :T].unsqueeze(1).to_broadcast([T, NT, T]),
                       dinv[:, :].unsqueeze(2).to_broadcast([T, NT, T]), ALU.mult).then_inc(diag_ready, 1)
                    dve.wait_ge(wr_hi, 2)
                    w3 = wr_p[0][:, 0:KD * 2 * EXP].rearrange("p (k e) -> p k e", e=2 * EXP)
                    tt(w3[:, :, EXP:], wr_raw[:, :].rearrange("p (k e) -> p k e", e=EXP),
                       w3[:, :, 0:EXP].bitcast(F32), ALU.subtract).then_inc(wr_lo, 1)
                elif kind == "ZP":
                    _, layer, t = k
                    s_, n = t % 2, (layer - 1) * KD + t
                    dve.wait_ge(xs_landed[s_], 16 * (n // 2 + 1))
                    raw = xs_raw[s_][:, :, :]
                    tt(raw, raw, dinv[:, :].unsqueeze(2).to_broadcast([T, NT, 128]), ALU.mult
                       ).then_inc(xs_scaled, 1)
                    dve.wait_ge(act_done, ACTED[k])
                    tt(xs_p[s_][1][:, :, :], raw, xs_p[s_][0][:, :, :].bitcast(F32), ALU.subtract
                       ).then_inc(dve_done, 1)
                elif kind == "Z":
                    _, layer, t = k
                    dve.wait_ge(psum_full, u)
                    dve.wait_ge(act_done, ACTED[("DB",)])
                    tt(chunks(ztmp[t % 2][:, :]), cols(ps), chunks(dinv_b[:, :]), ALU.mult).then_inc(z_scaled, 1)
                    dve.wait_ge(act_done, ACTED[k])
                    tt(big[1][:, t, :], ztmp[t % 2][:, :], big[0][:, t, :].bitcast(F32), ALU.subtract
                       ).then_inc(dve_done, 1)
                elif kind == "P":
                    n = k[1]
                    dve.wait_ge(act_done, ACTED[k])
                    tt(slab_p[n % 2][1][:, :, :].rearrange("p k c -> p (k c)"), slab_raw[n % 2][:, :],
                       slab_p[n % 2][0][:, :, :].bitcast(F32).rearrange("p k c -> p (k c)"), ALU.subtract
                       ).then_inc(dve_done, 1)
                elif kind == "H":
                    if k[1] == 2:
                        continue
                    f = k[2]
                    h = htmp[f % 2]
                    dve.wait_ge(h_biased, f + 1)
                    for q in range(3):
                        a = q * CW
                        ins = dve.bn_stats(bst[:, 6 * q:6 * q + 6], h[:, a:min(a + CW, N)])
                    link(ins)
                    dve.bn_aggr(bmv[:, :], bst[:, :].rearrange("p (q c) -> p q c", c=6)).then_inc(bn_ready, 1)
                    dve.wait_ge(std_ready, f + 1)
                    link(ts(nw[:, 0:1], bmv[:, 1:2], BN_EPS, ALU.add))
                    link(newton(nw[:, 1:2], nw[:, 0:1], std[:, 0:1], 1, 128, nw[:, 2:4]))
                    link(tt(bsc[:, 0:1], nw[:, 1:2], gammac[:, f:f + 1], ALU.mult))
                    link(tt(nw[:, 4:5], bmv[:, 0:1], bsc[:, 0:1], ALU.mult))
                    tt(bsc[:, 1:2], betac[:, f:f + 1], nw[:, 4:5], ALU.subtract).then_inc(bn_affine, 1)
                elif kind in ("XT", "FT"):
                    i = k[1]
                    dve.wait_ge(act_done, ACTED[k])
                    tt(big[1][:, :, T * i:T * i + T], blocks(ps, KD, T, 128),
                       big[0][:, :, T * i:T * i + T].bitcast(F32), ALU.subtract).then_inc(dve_done, 1)
                elif kind == "VT":
                    dve.wait_ge(act_done, ACTED[k])
                    tt(v_cols(v_p[1][:, :, :]), v_psum(ps), v_cols(v_p[0][:, :, :].bitcast(F32)), ALU.subtract
                       ).then_inc(dve_done, 1)
                elif kind in ("K", "Q"):
                    parts = k_p if kind == "K" else q_p
                    dve.wait_ge(act_done, ACTED[k])
                    tt(chunks(parts[1][:, :]), cols(ps), chunks(parts[0][:, :].bitcast(F32)), ALU.subtract
                       ).then_inc(dve_done, 1)
                elif kind == "KK":
                    dve.wait_ge(act_done, ACTED[k])
                    dve.scalar_tensor_tensor(
                        out=kk_p[k[2] % 3][1][:, :], in0=ps[:T, :2 * FEAT], scalar=0.0,
                        in1=kk_p[k[2] % 3][0][:, :].bitcast(F32), op0=ALU.max, op1=ALU.subtract
                    ).then_inc(dve_done, 1)
                elif kind == "S":
                    dve.wait_ge(act_done, ACTED[k])
                    tt(s_p[1][:, :, :, :].rearrange("p h f c -> p (h f c)"), lsb[:, :],
                       s_p[0][:, :, :, :].bitcast(F32).rearrange("p h f c -> p (h f c)"), ALU.subtract
                       ).then_inc(dve_done, 1)
                elif kind == "MP":
                    dve.wait_ge(act_done, ACTED[k])
                    tt(proj_p[1][:, :], proj_raw[:, :], proj_p[0][:, :].bitcast(F32), ALU.subtract
                       ).then_inc(dve_done, 1)
                elif kind == "QP":
                    dve.wait_ge(act_done, ACTED[k])
                    dve.scalar_tensor_tensor(
                        out=chunks(qp_p[1][:, k[3], :]), in0=cols(ps), scalar=0.0,
                        in1=chunks(qp_p[0][:, k[3], :].bitcast(F32)), op0=ALU.max, op1=ALU.subtract
                    ).then_inc(dve_done, 1)
                elif kind == "RC":
                    p = k[1]
                    dve.wait_ge(act_done, ACTED[("AT", p, 1)])
                    link(dve.reciprocal(nrm[:, :], nrm[:, :]))
                    tt(num[:, :], num[:, :], nrm[:, :], ALU.mult).then_inc(dve_done, 1)
                elif kind == "RH":
                    p = k[1]
                    dve.wait_ge(act_done, ACTED[k])
                    if 0 < p < PAIRS - 1:
                        dve.wait_ge(att_stored, 32 * p)
                    hi, lo = (att_p[q][:, :] if p < PAIRS - 1 else big[q][:, p, :] for q in range(2))
                    tt(lo, num[:, :], hi.bitcast(F32), ALU.subtract).then_inc(dve_done, 1)
                elif kind == "O":
                    f = k[1]
                    dve.wait_ge(psum_full, u)
                    dve.wait_ge(gnn_landed[f % 2], 16 * (f // 2 + 1))
                    dve.scalar_tensor_tensor(out=chunks(otmp[f % 2][:, :]), in0=cols(ps), scalar=boc[:, f:f + 1],
                                             in1=chunks(gnn_in[f % 2][:, :]), op0=ALU.add, op1=ALU.add
                                             ).then_inc(dve_done, 1)
                elif kind == "OT":
                    f = k[1]
                    dve.wait_ge(psum_full, u)
                    dve.wait_ge(xr_landed[f % 2], 16 * (f // 2 + 1))
                    tt(acc[:, :, 128 * f:128 * f + 128], blocks(ps, NT, 128, T), x_in[f % 2][:, :, :], ALU.add
                       ).then_inc(dve_done, 1)
                    dve.wait_ge(dve_done, DVED[k])
                    for j in range(NT):
                        ins = dve.bn_stats(l2st[:, j, 6 * f:6 * f + 6], acc[:, j, 128 * f:128 * f + 128])
                    if f == KD - 1:
                        link(ins)
                elif kind == "LN2":
                    for j in range(NT):
                        ins = dve.bn_aggr(l2mv[:, 2 * j:2 * j + 2], l2st[:, j, :].rearrange("p (q c) -> p q c", c=6))
                    link(ins)
                    ts(nw[:T, 0:NT], l2mv[:, 1:2 * NT:2], LN_EPS, ALU.add).then_inc(ln2_var, 1)
                    dve.wait_ge(ln2_std, 1)
                    dve.wait_ge(ln2_var, 1)
                    link(newton(rstd[:, :], nw[:T, 0:NT], std[:T, :], NT, T, nw[:, NT:3 * NT]))
                elif kind == "FL":
                    j = k[1]
                    if j >= 2:
                        dve.wait_ge(psum_full, FULL[("FT", j - 2)])
                        dve.wait_ge(flat_stored[j % 2], 16 * (j // 2))
                    ts(flat[j % 2][:, :], acc[:, j, :], l2mv[:, 2 * j:2 * j + 1], ALU.subtract,
                       rstd[:, j:j + 1], ALU.mult).then_inc(dve_done, 1)
                elif kind == "RT":
                    dve.wait_ge(act_done, ACTED[k])
                    dve.wait_ge(const_in, 16 * 4)
                    l_, rk, rt = lg[:, :, :], rank[:, :, :], rtmp[:, :, :]
                    two = lg2[:, :].rearrange("p (j e) -> p j e", e=2 * EXP)
                    link(tt(l_, two[:, :, 0:EXP], two[:, :, EXP:], ALU.add))
                    sh = [T, NT, EXP, EXP]
                    g4 = cmp_gt[:, :, :].rearrange("p j (e o) -> p j e o", o=EXP)
                    h4 = cmp_ge[:, :, :].rearrange("p j (e o) -> p j e o", o=EXP)
                    me, other = l_.unsqueeze(3).to_broadcast(sh), l_.unsqueeze(2).to_broadcast(sh)
                    tt(g4, other, me, ALU.is_gt)
                    link(tt(h4, other, me, ALU.is_equal))
                    link(tt(cmp_ge[:, :, :], cmp_ge[:, :, :],
                            tie_t[:, :].unsqueeze(1).to_broadcast([T, NT, EXP * EXP]), ALU.mult))
                    link(tt(cmp_gt[:, :, :], cmp_gt[:, :, :], cmp_ge[:, :, :], ALU.add))
                    link(dve.tensor_reduce(rk, g4, AX.X, ALU.add))
                    m1, m2, df, ex, w1, w2_ = (rsm[:, NT * i:NT * i + NT] for i in range(6))
                    dve.tensor_reduce(m1, l_, AX.X, ALU.max)
                    link(ts(rt, rk, 1.0, ALU.is_equal))
                    link(tt(rt, rt, l_, ALU.mult))
                    link(dve.tensor_reduce(m2, rt, AX.X, ALU.add))
                    tt(df, m2, m1, ALU.subtract).then_inc(exp_in, 1)
                    dve.wait_ge(exp_out, 1)
                    link(ts(w2_, ex, 1.0, ALU.add))
                    link(dve.reciprocal(w1, w2_))
                    link(tt(w2_, ex, w1, ALU.mult))
                    bc = lambda a: a.unsqueeze(2).to_broadcast([T, NT, EXP])
                    rw3 = rw[:, :].rearrange("p (j e) -> p j e", e=EXP)
                    ts(rt, rk, 1.0, ALU.is_equal)
                    ts(sel[:, :], rk.rearrange("p j e -> p (j e)"), 1.5, ALU.is_lt).then_inc(sel_ready, 1)
                    link(ts(rw3, rk, 0.0, ALU.is_equal))
                    tt(rt, rt, bc(w2_), ALU.mult)
                    link(tt(rw3, rw3, bc(w1), ALU.mult))
                    tt(rw3, rw3, rt, ALU.add).then_inc(dve_done, 1)
                elif kind == "PX":
                    dve.wait_ge(psum_full, u)
                    dve.wait_ge(dve_done, DVED[("RT",)])
                    rt = rtmp[:, :, :].rearrange("p j e -> p (j e)")
                    link(ts(rt, rank[:, :, :].rearrange("p j e -> p (j e)"), 1.5, ALU.is_gt,
                            float(4 * CAP * ROUNDS), ALU.mult))
                    tt(pos[:, :], rt, ps[:T, 0:NT * EXP], ALU.add)
                    longest, more = nw[0:1, 0:1], nw[0:1, 1:2]
                    link(dve.tensor_reduce(longest, ps[0:1, 512:512 + EXP], AX.X, ALU.max))
                    link(ts(more, longest, float(CAP), ALU.is_gt, 1.0, ALU.add))
                    for n in range(2, ROUNDS):
                        link(dve.scalar_tensor_tensor(out=more, in0=longest, scalar=float(CAP * n), in1=more,
                                                      op0=ALU.is_gt, op1=ALU.add))
                    dve.tensor_copy(rounds_n[:, :], more).then_inc(rounds_ready, 1)
                    r3 = rec[:, :, :, :].rearrange("p j e c -> p (j e) c")
                    for c in range(3):
                        dve.tensor_copy(rec[:, :, :, c], tok_t[:, :, c:c + 1].to_broadcast([T, NT, EXP]))
                    link(dve.tensor_copy(r3[:, :, 3], rw[:, :]))
                    link(tt(rt, rw[:, :], r3[:, :, 3], ALU.subtract))
                    link(dve.tensor_copy(r3[:, :, 4], rt))
                    link(tt(rt, rt, r3[:, :, 4], ALU.subtract))
                    dve.tensor_copy(r3[:, :, 5], rt).then_inc(dve_done, 1)

            dve.wait_ge(rounds_ready, 1)
            dve.wait_ge(dve_done, DVED[("PX",)])
            rounds = dve.value_load(rounds_n[0:1, 0:1], min_val=1, max_val=ROUNDS)
            with dve.Fori(0, rounds) as r:
                r_links = [0]
                LINKS = 7 * EXP + 1

                def r_link(ins):
                    r_links[0] += 1
                    ins.then_inc(round_chain, 1)
                    dve.wait_ge(round_chain, r * LINKS + r_links[0])

                def acted(k):
                    dve.wait_ge(expert_act, r * len(R_ACT) + R_ACT[k])

                for k in ROUND:
                    kind = k[0]
                    if kind == "WP":
                        m = k[1]
                        acted(k)
                        tt(ws_p[m % 3][1][:, :, :].rearrange("p k c -> p (k c)"), ws_raw[m % 4][:, :],
                           ws_p[m % 3][0][:, :, :].bitcast(F32).rearrange("p k c -> p (k c)"), ALU.subtract
                           ).then_inc(expert_dve, 1)
                    elif kind == "W2P":
                        p_ = w2_p[k[1] % 2]
                        acted(k)
                        tt(p_[1][:, :, :], w2_raw[:, :, :], p_[0][:, :, :].bitcast(F32), ALU.subtract
                           ).then_inc(expert_dve, 1)
                    elif kind == "LD":
                        e = k[1]
                        if e:
                            dve.wait_ge(expert_full, r * len(R_FULL) + R_FULL[("LS", e - 1)])
                            dve.wait_ge(expert_dve, r * len(R_DVE) + R_DVE[("LS", e - 1)])
                        for j in range(NT):
                            c = EXP * j + e
                            ins = ts(hit[:, j, :], place_iota[:, :], pos[:, c:c + 1], ALU.is_equal)
                        ins.then_inc(hits_ready, 1)
                    elif kind == "LS":
                        e = k[1]
                        dve.wait_ge(expert_full, r * len(R_FULL) + R_FULL[k])
                        if e >= 4:
                            dve.wait_ge(added, r * (16 * NRT * EXP) + 16 * NRT * (e - 3))
                        got = lsb[:RT_, 0:8 * NRT].rearrange("p (i c) -> p i c", c=8)
                        r_link(ts(ls_a[:, :], got[:, :, 0], -1.0, ALU.mult, 1.0, ALU.add))
                        r_link(tt(ls_a[:, :], ls_a[:, :], place_no[:, :], ALU.mult))
                        r_link(tt(ls_a[:, :], ls_a[:, :], got[:, :, 1], ALU.add))
                        r_link(dve.scalar_tensor_tensor(out=ls_a[:, :], in0=got[:, :, 2], scalar=float(T),
                                                        in1=ls_a[:, :], op0=ALU.mult, op1=ALU.add))
                        r_link(dve.tensor_copy(ls_b[:, :], got[:, :, 5]))
                        r_link(tt(ls_b[:, :], ls_b[:, :], got[:, :, 4], ALU.add))
                        r_link(tt(share[e % 4][:, :], ls_b[:, :], got[:, :, 3], ALU.add))
                        dve.tensor_copy(token[e % 4][:, :], ls_a[:, :]).then_inc(expert_dve, 1)
                    elif kind == "XE":
                        e, i = k[1:]
                        acted(k)
                        at_ = slice(RT_ * i, RT_ * i + RT_)
                        tt(xe_p[e % 2][1][:, :, at_], blocks(wide[(WIDE[k] - 1) % 2], KD, RT_, 128),
                           xe_p[e % 2][0][:, :, at_].bitcast(F32), ALU.subtract).then_inc(expert_dve, 1)
                    elif kind == "VA":
                        e, t = k[1:]
                        n = 2 * e + t
                        dve.wait_ge(expert_full, r * len(R_FULL) + R_FULL[k])
                        acted(("GA", e, t))
                        if n:
                            dve.wait_ge(expert_dve, r * len(R_DVE) + R_DVE[("VA", (n - 1) // 2, (n - 1) % 2)])
                        tt(actt[:, :], narrow[(NARROW[k] - 1) % 3], sil[:, :], ALU.mult
                           ).then_inc(act_made, 1)
                        acted(k)
                        tt(a_p[1][:, t, :], actt[:, :], a_p[0][:, t, :].bitcast(F32), ALU.subtract
                           ).then_inc(expert_dve, 1)
                r_link(ts(pos[:, :], pos[:, :], float(CAP), ALU.subtract))
                dve.wait_ge(added, (r + 1) * (16 * NRT * EXP))

        @block.tensor
        def _(ten):
            def free_slot(k):
                u = FULL[k] - 1
                if u >= 2:
                    before = UNITS[u - 2]
                    if before[0] == "H" and before[1] == 1:
                        ten.wait_ge(h_biased, before[2] + 1)
                    elif before[0] in LAST_READER_DVE:
                        if before[0] == "Z":
                            ten.wait_ge(z_scaled, (before[1] - 1) * KD + before[2] + 1)
                        else:
                            ten.wait_ge(dve_done, DVED[before])
                    else:
                        ten.wait_ge(act_done, ACTED[before])

            def slab_product(k, ps):
                n = SLAB[k]
                ten.wait_ge(dve_done, DVED[("P", n)])
                w = slab_p[n % 2]
                for kt in range(KD):
                    if k[0] == "O" and k[1] == 0 and kt == 0:
                        ten.wait_ge(at_landed, 32 * (PAIRS - 1))
                    if k[0] == "O" and k[1] == 0 and kt == KD - 1:
                        ten.wait_ge(dve_done, DVED[("RH", PAIRS - 1)])
                    for c, (a, b) in enumerate(COMBOS):
                        for q in range(3):
                            mm = ten.matmul(ps[:, 512 * q:512 * q + CW], w[a][:, kt, :],
                                            big[b][:, kt, CW * q:CW * q + CW],
                                            start=(kt == 0 and c == 0), stop=(kt == KD - 1 and c == 2))
                return mm

            start = 0
            for k in ORDER:
                kind = k[0]
                if kind not in PSUM_KINDS and kind not in ("KV", "S"):
                    continue
                if kind in PSUM_KINDS:
                    ps = slot[slot_of(k)]
                    free_slot(k)
                if kind == "G":
                    b = k[1]
                    if b == 0:
                        ten.wait_ge(memset_done, 5)
                        ten.wait_ge(bounds_ready, 1)
                        for j in range(GC):
                            ten.sem_inc(oh_used[j], 1)
                    end = ten.value_load(bounds[0:1, b:b + 1], min_val=1, max_val=NG * NT)
                    span = [(512 * q, CW * q, min(CW, N - CW * q)) for q in range(3)]
                    for to, at_, w in span:
                        ten.matmul(ps[:T, to:to + w], zeros[:T, :T], iota_t[:, at_:at_ + w],
                                   start=True, stop=False, skip_group_check=True)
                    with ten.Fori(start, end) as r:
                        for j in range(GC):
                            ten.wait_ge(oh_ready[j], r + 1)
                            for q, (to, at_, w) in enumerate(span):
                                mm = ten.matmul(ps[:T, to:to + w], oh_dst[j][:, :], oh_src[j][:, at_:at_ + w],
                                                start=False, stop=False, skip_group_check=True)
                            mm.then_inc(oh_used[j], 1)
                    for to, at_, w in span:
                        mm = ten.matmul(ps[:T, to:to + w], zeros[:T, :T], iota_t[:, at_:at_ + w],
                                        start=False, stop=True, skip_group_check=True)
                    start = end
                elif kind == "GT":
                    b = k[1]
                    ten.wait_ge(diag_added, b + 1)
                    for j in range(NT):
                        mm = ten.transpose(ps[:T, 128 * j:128 * j + T], cnt[b % 2][:, T * j:T * j + T],
                                           ident[:T, :T])
                elif kind == "DB":
                    ten.wait_ge(diag_ready, 1)
                    for j in range(NT):
                        mm = ten.matmul(ps[:, 128 * j:128 * j + T], onesf[:T, :], diag[:, j, :],
                                        start=True, stop=True)
                elif kind == "Z":
                    _, layer, t = k
                    ten.wait_ge(dve_done, DVED[("ZP", layer, t)])
                    for j in range(NT):
                        for a in range(2):
                            for q in range(3):
                                mm = ten.matmul(ps[:, 512 * q:512 * q + CW], xs_p[t % 2][a][:, j, :],
                                                adj[:, j, CW * q:CW * q + CW],
                                                start=(j == 0 and a == 0), stop=(j == NT - 1 and a == 1))
                elif kind in ("H", "V", "K", "Q", "O"):
                    if kind == "H" and k[2] == 0:
                        ten.wait_ge(dve_done, DVED[("Z", k[1], KD - 1)])
                    if kind == "Q" and k[1] == 0:
                        ten.wait_ge(dve_done, DVED[("MP",)])
                    if kind == "V" and k[1] == 0:
                        ten.wait_ge(dve_done, DVED[("XT", NT - 1)])
                    mm = slab_product(k, ps)
                elif kind in ("HT", "VT", "OT"):
                    if kind == "HT":
                        src_t = htmp[k[1] % 2]
                        ten.wait_ge(act_done, ACTED[("H", 1, k[1])])
                    elif kind == "VT":
                        src_t = vt
                        ten.wait_ge(act_done, ACTED[("V", k[1])])
                    else:
                        src_t = otmp[k[1] % 2]
                        ten.wait_ge(dve_done, DVED[("O", k[1])])
                    for j in range(NT):
                        mm = ten.transpose(ps[:T, 128 * j:128 * j + 128], src_t[:, T * j:T * j + T], ident[:, :])
                elif kind in ("XT", "FT"):
                    i = k[1]
                    if kind == "XT":
                        src_t = xn_in[i % 2]
                        ten.wait_ge(xn_landed[i % 2], 16 * (i // 2 + 1))
                    else:
                        src_t = flat[i % 2]
                        ten.wait_ge(dve_done, DVED[("FL", i)])
                    for j in range(KD):
                        mm = ten.transpose(ps[:, 128 * j:128 * j + T], src_t[:, 128 * j:128 * j + 128],
                                           ident[:T, :T])
                elif kind == "KK":
                    p, i = k[1], k[2]
                    if i == 0:
                        ten.wait_ge(dve_done, DVED[("K", p)])
                    for c, (a, b) in enumerate(COMBOS):
                        mm = ten.matmul(ps[:T, :2 * FEAT], k_p[a][:, T * i:T * i + T], proj_p[b][:, :],
                                        start=(c == 0), stop=(c == 2))
                elif kind == "KV":
                    p, i = k[1], k[2]
                    ten.wait_ge(dve_done, DVED[("KK", p, i)])
                    if i == 0:
                        ten.wait_ge(dve_done, DVED[("VT", p)])
                        if p:
                            ten.wait_ge(act_done, ACTED[("KC", p - 1)])
                    for h in range(2):
                        for c, (a, b) in enumerate(COMBOS):
                            mm = ten.matmul(kvb[:, FEAT * h:FEAT * h + FEAT], v_p[a][:, i, 128 * h:128 * h + 128],
                                            kk_p[i % 3][b][:, FEAT * h:FEAT * h + FEAT],
                                            start=(i == 0 and h == 0 and c == 0), stop=(i == NT - 1),
                                            skip_group_check=True)
                    if i == NT - 1:
                        mm.then_inc(kv_full, 1)
                    continue
                elif kind == "S":
                    ten.wait_ge(act_done, ACTED[("KC", k[1])])
                    if k[1]:
                        ten.wait_ge(dve_done, DVED[("S", k[1] - 1)])
                    for q in range(4):
                        mm = ten.transpose(lsb[:, 128 * q:128 * q + 128], kvt[:, 128 * q:128 * q + 128], ident[:, :])
                    mm.then_inc(s_full, 1)
                    continue
                elif kind == "QP":
                    p, h, f = k[1:]
                    if h == 0 and f == 0:
                        ten.wait_ge(dve_done, DVED[("Q", p)])
                    o = FEAT * h + 128 * f
                    for c, (a, b) in enumerate(COMBOS):
                        for q in range(3):
                            mm = ten.matmul(ps[:, 512 * q:512 * q + CW], proj_p[a][:, o:o + 128],
                                            q_p[b][:, CW * q:CW * q + CW], start=(c == 0), stop=(c == 2))
                elif kind == "AT":
                    p, h = k[1], k[2]
                    ten.wait_ge(dve_done, DVED[("S", p)])
                    ten.wait_ge(dve_done, DVED[("QP", p, h, 1)])
                    for f in range(2):
                        for c, (a, b) in enumerate(COMBOS):
                            for q in range(3):
                                mm = ten.matmul(ps[:, 512 * q:512 * q + CW], s_p[a][:, h, f, :],
                                                qp_p[b][:, f, CW * q:CW * q + CW],
                                                start=(f == 0 and c == 0), stop=(f == 1 and c == 2))
                elif kind == "R":
                    ten.wait_ge(dve_done, DVED[("FT", NT - 1)])
                    for kt in range(KD):
                        for a in range(2):
                            for q in range(3):
                                mm = ten.matmul(ps[:, 512 * q:512 * q + CW],
                                                wr_p[a][:, 2 * EXP * kt:2 * EXP * kt + 128],
                                                big[a][:, kt, CW * q:CW * q + CW],
                                                start=(kt == 0 and a == 0), stop=(kt == KD - 1 and a == 1))
                elif kind == "RT":
                    ten.wait_ge(act_done, ACTED[("R",)])
                    for j in range(NT):
                        mm = ten.transpose(ps[:T, 2 * EXP * j:2 * EXP * j + 2 * EXP], lgt[:, T * j:T * j + T],
                                           ident[:2 * EXP, :2 * EXP])
                elif kind == "PX":
                    ten.wait_ge(sel_ready, 1)
                    ten.wait_ge(lists_in, 16 * 4)
                    ten.matmul(ps[:T, 0:NT * EXP], before_t[:, 0:T], sel[:, :], start=True, stop=False,
                               skip_group_check=True)
                    for j in range(NT - 1):
                        ten.matmul(ps[:T, EXP * (j + 1):NT * EXP].rearrange("p (j e) -> p j e", e=EXP),
                                   before_t[:, T:],
                                   sel[:, EXP * j:EXP * j + EXP].unsqueeze(1).to_broadcast([T, NT - 1 - j, EXP]),
                                   start=False, stop=(j == NT - 2), skip_group_check=True)
                    for j in range(NT):
                        mm = ten.matmul(ps[:T, 512:512 + EXP], before_t[:, T:], sel[:, EXP * j:EXP * j + EXP],
                                        start=(j == 0), stop=(j == NT - 1))
                mm.then_inc(psum_full, 1)

            ten.wait_ge(rounds_ready, 1)
            ten.wait_ge(dve_done, DVED[("PX",)])
            rounds = ten.value_load(rounds_n[0:1, 0:1], min_val=1, max_val=ROUNDS)
            with ten.Fori(0, rounds) as r:

                def dved(k):
                    ten.wait_ge(expert_dve, r * len(R_DVE) + R_DVE[k])

                def acted(k):
                    ten.wait_ge(expert_act, r * len(R_ACT) + R_ACT[k])

                for k in ROUND:
                    kind = k[0]
                    if kind in ("XE", "OUT"):
                        n = WIDE[k] - 1
                        ps = wide[n % 2]
                        if n >= 2:
                            before_ = WIDE_KEYS[n - 2]
                            (dved if before_[0] == "XE" else acted)(before_)
                    if kind == "LS":
                        e = k[1]
                        ten.wait_ge(hits_ready, r * EXP + e + 1)
                        if e:
                            dved(("LS", e - 1))
                        for j in range(NT):
                            for i in range(NRT):
                                mm = ten.matmul(lsb[:RT_, 8 * i:8 * i + 6], hit[:, j, RT_ * i:RT_ * i + RT_],
                                                rec[:, j, e, :], start=(j == 0 and i == 0), stop=(j == NT - 1),
                                                skip_group_check=True)
                    elif kind == "XE":
                        e, i = k[1:]
                        ten.wait_ge(gathered[e % 2][i], r * (16 * EXP // 2) + 16 * (e // 2 + 1))
                        for j in range(KD):
                            mm = ten.transpose(ps[:, 128 * j:128 * j + RT_], xg[e % 2][:, i, 128 * j:128 * j + 128],
                                               ident[:RT_, :RT_])
                    elif kind in ("GA", "VA"):
                        m = NARROW[k] - 1
                        ps = narrow[m % 3]
                        if m >= 3:
                            before_ = NARROW_KEYS[m - 3]
                            if before_[0] == "GA":
                                acted(before_)
                            else:
                                ten.wait_ge(act_made, r * (2 * EXP) + 2 * before_[1] + before_[2] + 1)
                        dved(("WP", m))
                        if kind == "GA" and k[2] == 0:
                            dved(("XE", k[1], NRT - 1))
                        w, xe = ws_p[m % 3], xe_p[k[1] % 2]
                        for kt in range(KD):
                            for c, (a, b) in enumerate(COMBOS):
                                mm = ten.matmul(ps, w[a][:, kt, :], xe[b][:, kt, :],
                                                start=(kt == 0 and c == 0), stop=(kt == KD - 1 and c == 2))
                    elif kind == "OUT":
                        e, i = k[1:]
                        if i == 0:
                            dved(("VA", e, 1))
                            dved(("W2P", e))
                        for f in range(HALVES):
                            for c, (a, b) in enumerate(COMBOS):
                                for q in range(2):
                                    mm = ten.matmul(ps[:RT_, 512 * q:512 * q + 512],
                                                    a_p[a][:, f, RT_ * i:RT_ * i + RT_],
                                                    w2_p[e % 2][b][:, f, 512 * q:512 * q + 512],
                                                    start=(f == 0 and c == 0), stop=(f == 1 and c == 2))
                    else:
                        continue
                    mm.then_inc(expert_full, 1)
                ten.wait_ge(expert_act, (r + 1) * len(R_ACT))
                ten.wait_ge(expert_dve, (r + 1) * len(R_DVE))


UNITS = [k for k in ORDER if k[0] in PSUM_KINDS]
LAST_READER_DVE = {"Z", "XT", "FT", "VT", "K", "Q", "KK", "QP", "O", "OT", "PX"}


def encoding():
    pos = np.arange(N, dtype=np.float32)[:, None]
    div = np.exp(np.arange(0, D, 2, dtype=np.float32) * np.float32(-np.log(10000.0) / D)).astype(np.float32)
    ang = (pos * div).astype(np.float32)
    return np.stack([np.sin(ang), np.cos(ang)], axis=-1).reshape(N, D).astype(np.float32)


def kernel(x, src, dst, L0_gnn_W1, L0_gnn_b1, L0_gnn_gamma, L0_gnn_beta, L0_gnn_W2, L0_gnn_b2,
           L0_mix_Wq, L0_mix_Wk, L0_mix_Wv, L0_mix_proj, L0_mix_Wo, L0_mix_bo,
           L0_ffn_Wr, L0_ffn_W1, L0_ffn_W2):
    from concourse import bacc
    from concourse.bass_utils import run_bass_kernel_spmd

    def columns(w):
        return np.asarray(w).reshape(KD, 128, KD, 128).transpose(2, 1, 0, 3).reshape(KD, 128, D)

    by_name = {("H", 1): columns(L0_gnn_W1), ("H", 2): columns(L0_gnn_W2), "V": columns(L0_mix_Wv),
               "K": columns(L0_mix_Wk), "Q": columns(L0_mix_Wq), "O": columns(L0_mix_Wo)}
    w1 = np.asarray(L0_ffn_W1).reshape(EXP, 2, 2, 128, KD, 128).transpose(0, 1, 2, 5, 4, 3)
    w1 = w1.reshape(EXP, 2, 2, 128, D)
    w1 = np.stack([w1[key[1], int(key[0] == "GA"), key[2]] for key in NARROW_KEYS])

    def slab(key):
        return by_name[key[:2] if key[0] == "H" else key[0]][key[-1]]

    f = np.asarray
    as_cols = lambda v: f(v).reshape(KD, 128).T
    arrays = {
        "x": f(x),
        "src_cols": f(src).reshape(NCH, CH).T, "dst_cols": f(dst).reshape(NCH, CH).T,
        "dst_groups": f(dst).reshape(NG, GC * CH),
        "slabs": np.stack([slab(k) for k in SLABS]),
        "w2": f(L0_ffn_W2).reshape(EXP, D, 2, 128).transpose(0, 3, 2, 1).reshape(EXP, 128, 2 * D),
        "wr": f(L0_ffn_Wr).reshape(EXP, KD, 128).transpose(2, 1, 0).reshape(128, KD * EXP),
        "proj": f(L0_mix_proj),
        "feat_rows": np.concatenate([as_cols(v) for v in (L0_gnn_b1, L0_gnn_gamma, L0_gnn_beta, L0_gnn_b2,
                                                          L0_mix_bo)], axis=1),
        "consts": np.eye(128, dtype=np.float32),
        "group_no": np.concatenate([
            np.stack([np.arange(NG) + 1, NG - np.arange(NG)], axis=1),
            np.tile(np.arange(NT) * T, (NG, 1)), np.tile(np.arange(NT) * T + T, (NG, 1))], axis=1
        ).astype(np.float32),
        "tie": np.tile(np.tril(np.ones((EXP, EXP), np.float32), -1).reshape(1, -1), (T, 1)),
        "iota": np.tile(np.arange(N, dtype=np.float16)[None], (T, 1)),
        "pe": encoding(),
        "w1": w1,
        "blank": np.zeros((CAP, D), np.float32),
        "before": np.concatenate([np.triu(np.ones((T, T)), 1), np.ones((T, T))], axis=1).astype(np.float16),
        "places": (N + np.arange(CAP)).reshape(NRT, RT_).T.astype(np.float32),
        "tokens": np.stack([np.ones((T, NT)), np.tile(np.arange(T)[:, None], (1, NT)),
                            np.tile(np.arange(NT), (T, 1))], axis=2).reshape(T, NT * 3).astype(np.float32),
    }
    arrays = {k: np.ascontiguousarray(v) for k, v in arrays.items()}
    nc = bacc.Bacc("TRN2", target_bir_lowering=False, num_devices=1)
    args = {k: nc.dram_tensor(k + "_dram", v.shape, mybir.dt.from_np(v.dtype), kind="ExternalInput").ap()
            for k, v in arrays.items()}
    out = nc.dram_tensor("out_dram", (N + CAP, D), F32, kind="ExternalOutput").ap()
    build(nc, **args, out=out)
    r = run_bass_kernel_spmd(nc, [{k + "_dram": v for k, v in arrays.items()}], core_ids=[0])
    return r.results[0]["out_dram"][:N]
```
